# Optimizing a Trainium2 kernel written in Bass

```python
import numpy as np
import jax
import jax.numpy as jnp

def _softmax(x, axis=-1):
    return jax.nn.softmax(x, axis=axis)

def _gelu(x):
    return jax.nn.gelu(x, approximate=True)

def _silu(x):
    return jax.nn.silu(x)

def _sigmoid(x):
    return jax.nn.sigmoid(x)

def _layernorm(x, axis=-1, eps=1e-05):
    m = jnp.mean(x, axis=axis, keepdims=True)
    v = jnp.var(x, axis=axis, keepdims=True)
    return (x - m) / jnp.sqrt(v + eps)

def _scatter_add(tgt, idx, src, axis=0):
    return tgt.at[idx].add(src)

def _segment_sum(src, seg, n):
    return jax.ops.segment_sum(src, seg, n)
kernel_name = 'mk_adaln_d1_jaxref_r4_bf691c'

def setup_inputs(seed: int=0):
    np.random.seed(seed)
    _w = jnp.asarray

    def _L0_attn_setup():
        import jax, jax.numpy as jnp
        import numpy as np
        D_MODEL = 256
        N_HEADS = 32
        D_INNER = 2 * D_MODEL
        HEADDIM = D_INNER // N_HEADS
        D_STATE = 128
        D_CONV = 4
        CONV_DIM = D_INNER + 2 * D_STATE
        D_IN_PROJ = 2 * D_INNER + 2 * D_STATE + N_HEADS
        D_FF = 1024
        B, L = (2, 512)

        def layernorm(x, w, b, eps=1e-05):
            mu = jnp.mean(x, axis=-1, keepdims=True)
            var = jnp.mean(jnp.square(x - mu), axis=-1, keepdims=True)
            return (x - mu) * jax.lax.rsqrt(var + eps) * w + b

        def causal_conv1d(x, w, b):
            K = w.shape[1]
            xp = jnp.pad(x, ((0, 0), (K - 1, 0), (0, 0)))
            Ln = x.shape[1]
            y = b
            for k in range(K):
                y = y + xp[:, k:k + Ln, :] * w[:, k]
            return y

        def ssd_scan(xh, dt, Bm, Cm, A):
            dA = jnp.exp(dt * A)
            dBx = dt[..., None] * xh
            b, l, h, p = xh.shape
            n = Bm.shape[-1]

            def step(hst, inp):
                dA_t, dBx_t, B_t, C_t = inp
                hst = hst * dA_t[:, :, None, None] + dBx_t[..., None] * B_t[:, None, None, :]
                y = jnp.einsum('bhpn,bn->bhp', hst, C_t)
                return (hst, y)
            xs = (jnp.moveaxis(dA, 1, 0), jnp.moveaxis(dBx, 1, 0), jnp.moveaxis(Bm, 1, 0), jnp.moveaxis(Cm, 1, 0))
            h0 = jnp.zeros((b, h, p, n), dtype=xh.dtype)
            _, ys = jax.lax.scan(step, h0, xs)
            return jnp.moveaxis(ys, 0, 1)

        def mamba2_mixer(xn, in_proj_w, conv_w, conv_b, dt_bias, A_log, D_skip, rms_w, out_proj_w):
            zxbcdt = xn @ in_proj_w
            z = zxbcdt[..., :D_INNER]
            xBC = zxbcdt[..., D_INNER:D_INNER + CONV_DIM]
            dt = zxbcdt[..., D_INNER + CONV_DIM:]
            dt = jax.nn.softplus(dt + dt_bias)
            xBC = jax.nn.silu(causal_conv1d(xBC, conv_w, conv_b))
            x_ssm = xBC[..., :D_INNER]
            Bm = xBC[..., D_INNER:D_INNER + D_STATE]
            Cm = xBC[..., D_INNER + D_STATE:]
            A = -jnp.exp(A_log)
            xh = x_ssm.reshape(*x_ssm.shape[:-1], N_HEADS, HEADDIM)
            y = ssd_scan(xh, dt, Bm, Cm, A)
            y = y + D_skip[None, None, :, None] * xh
            y = y.reshape(*y.shape[:-2], D_INNER)
            y = y * jax.nn.silu(z)
            y = y * jax.lax.rsqrt(jnp.mean(jnp.square(y), axis=-1, keepdims=True) + 1e-05) * rms_w
            return y @ out_proj_w
        key = jax.random.key(seed)
        ks = jax.random.split(key, 12)
        s = 0.02
        dt = jnp.exp(jax.random.uniform(ks[1], (N_HEADS,)) * (np.log(0.1) - np.log(0.001)) + np.log(0.001))
        dt_bias = dt + jnp.log(-jnp.expm1(-dt))
        return {'x': jax.random.normal(ks[0], (B, L, D_MODEL), jnp.float32), 'ln_w': jnp.ones((D_MODEL,), jnp.float32), 'ln_b': jnp.zeros((D_MODEL,), jnp.float32), 'in_proj_w': jax.random.normal(ks[2], (D_MODEL, D_IN_PROJ), jnp.float32) * s, 'conv_w': jax.random.normal(ks[3], (CONV_DIM, D_CONV), jnp.float32) * 0.3, 'conv_b': jnp.zeros((CONV_DIM,), jnp.float32), 'dt_bias': dt_bias.astype(jnp.float32), 'A_log': jnp.log(jax.random.uniform(ks[4], (N_HEADS,), minval=1.0, maxval=16.0)).astype(jnp.float32), 'D_skip': jnp.ones((N_HEADS,), jnp.float32), 'rms_w': jnp.ones((D_INNER,), jnp.float32), 'out_proj_w': jax.random.normal(ks[5], (D_INNER, D_MODEL), jnp.float32) * s, 'mlp_w1': jax.random.normal(ks[6], (D_MODEL, D_FF), jnp.float32) * s, 'mlp_b1': jnp.zeros((D_FF,), jnp.float32), 'mlp_w2': jax.random.normal(ks[7], (D_FF, D_MODEL), jnp.float32) * s, 'mlp_b2': jnp.zeros((D_MODEL,), jnp.float32)}
    _L0_attn_in = _L0_attn_setup()

    def _L0_ffn_setup():
        import jax, jax.numpy as jnp
        import numpy as np
        D_IN, D_HID = (256, 1024)

        def _ternary(key, shape):
            return jax.random.randint(key, shape, -1, 2).astype(jnp.float32)

        def _tlin(x, w, s):
            return jnp.einsum('bsi,oi->bso', x, w) * s
        key = jax.random.key(seed)
        ks = jax.random.split(key, 12)
        inv = lambda fan: 1.0 / np.sqrt(fan).astype(np.float32)
        return {'x': jax.random.normal(ks[0], (4, 512, D_IN), dtype=jnp.float32), 'w1_w': _ternary(ks[1], (D_HID, D_IN)), 'w1_s': jax.random.uniform(ks[2], (D_HID,), dtype=jnp.float32) * inv(D_IN), 'w2_w': _ternary(ks[3], (D_HID, D_IN)), 'w2_s': jax.random.uniform(ks[4], (D_HID,), dtype=jnp.float32) * inv(D_IN), 'h1_w': _ternary(ks[5], (D_HID, D_HID)), 'h1_s': jax.random.uniform(ks[6], (D_HID,), dtype=jnp.float32) * inv(D_HID), 'h2_w': _ternary(ks[7], (D_HID, D_HID)), 'h2_s': jax.random.uniform(ks[8], (D_HID,), dtype=jnp.float32) * inv(D_HID), 'w3_w': _ternary(ks[9], (D_IN, D_HID)), 'w3_s': jax.random.uniform(ks[10], (D_IN,), dtype=jnp.float32) * inv(D_HID)}
    _L0_ffn_in = _L0_ffn_setup()
    _L0_c = _w((lambda *s: np.random.randn(*s).astype(np.float32) * 0.05)(8, 256))
    _L0_wmod = _w((lambda *s: np.random.randn(*s).astype(np.float32) * 0.05)(256, 6 * 256) * 256 ** (-0.5))
    _d = {'L0_attn_x': _L0_attn_in['x'], 'L0_attn_ln_w': _L0_attn_in['ln_w'], 'L0_attn_ln_b': _L0_attn_in['ln_b'], 'L0_attn_in_proj_w': _L0_attn_in['in_proj_w'], 'L0_attn_conv_w': _L0_attn_in['conv_w'], 'L0_attn_conv_b': _L0_attn_in['conv_b'], 'L0_attn_dt_bias': _L0_attn_in['dt_bias'], 'L0_attn_A_log': _L0_attn_in['A_log'], 'L0_attn_D_skip': _L0_attn_in['D_skip'], 'L0_attn_rms_w': _L0_attn_in['rms_w'], 'L0_attn_out_proj_w': _L0_attn_in['out_proj_w'], 'L0_attn_mlp_w1': _L0_attn_in['mlp_w1'], 'L0_attn_mlp_b1': _L0_attn_in['mlp_b1'], 'L0_attn_mlp_w2': _L0_attn_in['mlp_w2'], 'L0_attn_mlp_b2': _L0_attn_in['mlp_b2'], 'L0_ffn_w1_w': _L0_ffn_in['w1_w'], 'L0_ffn_w1_s': _L0_ffn_in['w1_s'], 'L0_ffn_w2_w': _L0_ffn_in['w2_w'], 'L0_ffn_w2_s': _L0_ffn_in['w2_s'], 'L0_ffn_h1_w': _L0_ffn_in['h1_w'], 'L0_ffn_h1_s': _L0_ffn_in['h1_s'], 'L0_ffn_h2_w': _L0_ffn_in['h2_w'], 'L0_ffn_h2_s': _L0_ffn_in['h2_s'], 'L0_ffn_w3_w': _L0_ffn_in['w3_w'], 'L0_ffn_w3_s': _L0_ffn_in['w3_s'], 'L0_c': _L0_c, 'L0_wmod': _L0_wmod}
    _x0 = _d['L0_attn_x']
    _d['L0_attn_x'] = jax.random.normal(jax.random.fold_in(jax.random.key(seed), 1), (8, 1024, 256), dtype=_x0.dtype)
    del _x0
    return _d

def reference(L0_attn_x, L0_attn_ln_w, L0_attn_ln_b, L0_attn_in_proj_w, L0_attn_conv_w, L0_attn_conv_b, L0_attn_dt_bias, L0_attn_A_log, L0_attn_D_skip, L0_attn_rms_w, L0_attn_out_proj_w, L0_attn_mlp_w1, L0_attn_mlp_b1, L0_attn_mlp_w2, L0_attn_mlp_b2, L0_ffn_w1_w, L0_ffn_w1_s, L0_ffn_w2_w, L0_ffn_w2_s, L0_ffn_h1_w, L0_ffn_h1_s, L0_ffn_h2_w, L0_ffn_h2_s, L0_ffn_w3_w, L0_ffn_w3_s, L0_c, L0_wmod):

    def _L0_attn_ref(x, ln_w, ln_b, in_proj_w, conv_w, conv_b, dt_bias, A_log, D_skip, rms_w, out_proj_w, mlp_w1, mlp_b1, mlp_w2, mlp_b2):
        import jax, jax.numpy as jnp
        import numpy as np
        D_MODEL = 256
        N_HEADS = 32
        D_INNER = 2 * D_MODEL
        HEADDIM = D_INNER // N_HEADS
        D_STATE = 128
        D_CONV = 4
        CONV_DIM = D_INNER + 2 * D_STATE
        D_IN_PROJ = 2 * D_INNER + 2 * D_STATE + N_HEADS
        D_FF = 1024
        B, L = (2, 512)

        def layernorm(x, w, b, eps=1e-05):
            mu = jnp.mean(x, axis=-1, keepdims=True)
            var = jnp.mean(jnp.square(x - mu), axis=-1, keepdims=True)
            return (x - mu) * jax.lax.rsqrt(var + eps) * w + b

        def causal_conv1d(x, w, b):
            K = w.shape[1]
            xp = jnp.pad(x, ((0, 0), (K - 1, 0), (0, 0)))
            Ln = x.shape[1]
            y = b
            for k in range(K):
                y = y + xp[:, k:k + Ln, :] * w[:, k]
            return y

        def ssd_scan(xh, dt, Bm, Cm, A):
            dA = jnp.exp(dt * A)
            dBx = dt[..., None] * xh
            b, l, h, p = xh.shape
            n = Bm.shape[-1]

            def step(hst, inp):
                dA_t, dBx_t, B_t, C_t = inp
                hst = hst * dA_t[:, :, None, None] + dBx_t[..., None] * B_t[:, None, None, :]
                y = jnp.einsum('bhpn,bn->bhp', hst, C_t)
                return (hst, y)
            xs = (jnp.moveaxis(dA, 1, 0), jnp.moveaxis(dBx, 1, 0), jnp.moveaxis(Bm, 1, 0), jnp.moveaxis(Cm, 1, 0))
            h0 = jnp.zeros((b, h, p, n), dtype=xh.dtype)
            _, ys = jax.lax.scan(step, h0, xs)
            return jnp.moveaxis(ys, 0, 1)

        def mamba2_mixer(xn, in_proj_w, conv_w, conv_b, dt_bias, A_log, D_skip, rms_w, out_proj_w):
            zxbcdt = xn @ in_proj_w
            z = zxbcdt[..., :D_INNER]
            xBC = zxbcdt[..., D_INNER:D_INNER + CONV_DIM]
            dt = zxbcdt[..., D_INNER + CONV_DIM:]
            dt = jax.nn.softplus(dt + dt_bias)
            xBC = jax.nn.silu(causal_conv1d(xBC, conv_w, conv_b))
            x_ssm = xBC[..., :D_INNER]
            Bm = xBC[..., D_INNER:D_INNER + D_STATE]
            Cm = xBC[..., D_INNER + D_STATE:]
            A = -jnp.exp(A_log)
            xh = x_ssm.reshape(*x_ssm.shape[:-1], N_HEADS, HEADDIM)
            y = ssd_scan(xh, dt, Bm, Cm, A)
            y = y + D_skip[None, None, :, None] * xh
            y = y.reshape(*y.shape[:-2], D_INNER)
            y = y * jax.nn.silu(z)
            y = y * jax.lax.rsqrt(jnp.mean(jnp.square(y), axis=-1, keepdims=True) + 1e-05) * rms_w
            return y @ out_proj_w
        residual = x
        xn = layernorm(residual, ln_w, ln_b)
        y = mamba2_mixer(xn, in_proj_w, conv_w, conv_b, dt_bias, A_log, D_skip, rms_w, out_proj_w)
        out = y + residual
        h = layernorm(out, ln_w, ln_b)
        h = jax.nn.relu(h @ mlp_w1 + mlp_b1) @ mlp_w2 + mlp_b2
        return h + out

    def _L0_ffn_ref(x, w1_w, w1_s, w2_w, w2_s, h1_w, h1_s, h2_w, h2_s, w3_w, w3_s):
        import jax, jax.numpy as jnp
        import numpy as np
        D_IN, D_HID = (256, 1024)

        def _ternary(key, shape):
            return jax.random.randint(key, shape, -1, 2).astype(jnp.float32)

        def _tlin(x, w, s):
            return jnp.einsum('bsi,oi->bso', x, w) * s
        h = jax.nn.silu(_tlin(x, w1_w, w1_s)) * _tlin(x, w2_w, w2_s)
        h = jax.nn.gelu(_tlin(h, h1_w, h1_s), approximate=False)
        h = jax.nn.gelu(_tlin(h, h2_w, h2_s), approximate=False)
        return _tlin(h, w3_w, w3_s)
    x = L0_attn_x
    mod = (_silu(L0_c) @ L0_wmod).reshape(L0_c.shape[0], 6, 1, -1)
    sa, ca, ga, sb, cb, gb = (mod[:, 0], mod[:, 1], mod[:, 2], mod[:, 3], mod[:, 4], mod[:, 5])
    ga = (2 * (ga >= 0) - 1) * jnp.maximum(jnp.abs(ga), 0.25)
    gb = (2 * (gb >= 0) - 1) * jnp.maximum(jnp.abs(gb), 0.25)
    h = _layernorm(x, axis=-1) * (1 + ca) + sa
    x = x + ga * _L0_attn_ref(h, L0_attn_ln_w, L0_attn_ln_b, L0_attn_in_proj_w, L0_attn_conv_w, L0_attn_conv_b, L0_attn_dt_bias, L0_attn_A_log, L0_attn_D_skip, L0_attn_rms_w, L0_attn_out_proj_w, L0_attn_mlp_w1, L0_attn_mlp_b1, L0_attn_mlp_w2, L0_attn_mlp_b2)
    h = _layernorm(x, axis=-1) * (1 + cb) + sb
    x = x + gb * _L0_ffn_ref(h, L0_ffn_w1_w, L0_ffn_w1_s, L0_ffn_w2_w, L0_ffn_w2_s, L0_ffn_h1_w, L0_ffn_h1_s, L0_ffn_h2_w, L0_ffn_h2_s, L0_ffn_w3_w, L0_ffn_w3_s)
    return x

_drawn_inputs = setup_inputs


def setup_inputs(seed=0):
    import zlib

    import numpy as np

    out = dict(_drawn_inputs(seed))
    spreads = {'L0_attn_ln_w': (1.0, 0.2),
     'L0_attn_ln_b': (0.0, 0.1),
     'L0_attn_conv_b': (0.0, 0.1),
     'L0_attn_D_skip': (1.0, 0.2),
     'L0_attn_rms_w': (1.0, 0.2),
     'L0_attn_mlp_b1': (0.0, 0.1),
     'L0_attn_mlp_b2': (0.0, 0.1)}
    factors = {}
    for name, (base, spread) in spreads.items():
        noise = np.random.default_rng([zlib.crc32(name.encode()), seed]).standard_normal(out[name].shape)
        drawn = base * np.exp(spread * noise) if base else spread * noise
        out[name] = jnp.asarray(drawn.astype(out[name].dtype))
    for name, factor in factors.items():
        out[name] = (out[name] * factor).astype(out[name].dtype)
    return out
```

```python
from contextlib import ExitStack

import concourse.bass as bass
from concourse import mybir

ALU = mybir.AluOpType
ACT = mybir.ActivationFunctionType
AX = mybir.AxisListType
F32 = mybir.dt.float32
F32R = mybir.dt.float32r
BF16 = mybir.dt.bfloat16
I32 = mybir.dt.int32

P = 128
B, L, D = 8, 1024, 256
HALF = 512
NU = L // HALF
NC = HALF // P
KD = D // P
NH, HD, DS = 32, 16, 128
DI = NH * HD
QI = DI // P
HQ = P // HD
XM = (DI + 2 * DS) // P
CONV = DI + 2 * DS
TAPS = 4
ZX = 2 * DI + 2 * DS
FF = 1024
KF = FF // P
G4 = 4
NG = NH // G4
EPS = 1e-5
PROJ = (*range(QI, 2 * QI + 2), *range(QI))
SERIES = 7


START = 1


def start(eng, counts):
    for count in counts:
        for s in count.sems:
            eng.sem_inc(s, START)


class Handover:

    def __init__(self, sem, name, keys, slots, fills=1, uses=1, both=True):
        self.full_sems = [sem(f"{name}_full{i}") for i in range(slots)]
        self.free_sems = [sem(f"{name}_free{i}") for i in range(slots)] if both else None
        self.place = {k: (i % slots, i // slots) for i, k in enumerate(keys)}
        self.rounds = [len(range(i, len(keys), slots)) for i in range(slots)]
        self.fills, self.uses = fills, uses
        self.sems = self.full_sems + (self.free_sems or [])

    def slot(self, key):
        return self.place[key][0]

    def full(self, key):
        return self.full_sems[self.slot(key)]

    def free(self, key):
        return self.free_sems[self.slot(key)]

    def turn(self, b, key):
        s, n = self.place[key]
        return b * self.rounds[s] + n

    def filled(self, b, key):
        return (self.turn(b, key) + 1) * self.fills + START

    def filled_before(self, b, key):
        return self.turn(b, key) * self.fills + START

    def used(self, b, key):
        return (self.turn(b, key) + 1) * self.uses + START

    def used_before(self, b, key):
        return self.turn(b, key) * self.uses + START


class Count:

    def __init__(self, sem, name, per):
        self.sem, self.per = sem(name), per
        self.sems = [self.sem]

    def at(self, b, n):
        return b * self.per + n + START


class Steps(Count):

    def __init__(self, sem, name, per):
        super().__init__(sem, name, per)
        self.n = 0

    def mark(self, ins):
        ins.then_inc(self.sem, 1)
        self.n += 1
        return self.n

    def closed(self):
        assert self.n == self.per, (self.n, self.per)


def mamba_bank_order():
    for u in range(NU):
        yield from ((u, "nT", k) for k in range(KD))
        yield (u, "dt")
        yield from ((u, "in", m) for m in PROJ)
        yield (u, "dtw")
        yield (u, "dec")
        yield from ((u, "ec", q) for q in range(QI))
        yield (u, "xT", 0)
        yield (u, "bt", 0)
        for c in range(NC):
            if c + 1 < NC:
                yield (u, "xT", c + 1)
                yield (u, "bt", c + 1)
            yield (u, "st", c)
            if c:
                yield (u, "op", c - 1)
        yield (u, "op", NC - 1)
        yield from ((u, "mT", k) for k in range(KD))
        yield from ((u, "m1", m) for m in range(KF))
        yield from ((u, "m2", j) for j in range(NC // 2))


def ffn_bank_order():
    for u in range(NU):
        for m in range(KF):
            yield (u, "a", m)
            yield (u, "g", m)
        yield from ((u, "h1", m) for m in range(KF))
        yield from ((u, "h2", m) for m in range(KF))
        yield from ((u, "o", j) for j in range(NC // 2))


DVE_STEPS = 105


def build(nc, x, ln_w, ln_b, w_in, conv_w, conv_b, dt_bias, a_log, d_skip, rms_w, w_out, m1, b1, m2,
          b2, w1, s1, w2, s2, h1, sh1, h2, sh2, w3, s3, cT, wmod, out):
    top = ExitStack()
    with top:
        def sem(name):
            return top.enter_context(nc.semaphore(name))

        def keep(name, shape, dt=F32):
            return top.enter_context(nc.sbuf_tensor(name, shape, dt))

        mod_d = nc.dram_tensor("mod_d", [B, 6 * D], F32, kind="Internal").ap()
        x1_d = nc.dram_tensor("x1_d", [B, L, D], F32, kind="Internal").ap()
        ffn_d = [nc.dram_tensor(n, [P, k * n_], F32, kind="Internal").ap()
                 for n, k, n_ in (("w1_d", KD, FF), ("w2_d", KD, FF), ("h1_d", KF, FF),
                                  ("h2_d", KF, FF), ("w3_d", KF, D))]

        s_fill, s_const = sem("pool_constants"), sem("dve_constants")
        ident = keep("ident", [P, P])
        ones = keep("ones", [P, P])
        neg_half = keep("neg_half", [P, 4])

        g = dict(s_fill=s_fill, s_const=s_const, ident=ident, ones=ones, neg_half=neg_half, mod_d=mod_d, x1_d=x1_d, ffn_d=ffn_d, x=x,
                 ln_w=ln_w, ln_b=ln_b, w_in=w_in, conv_w=conv_w, conv_b=conv_b, dt_bias=dt_bias,
                 a_log=a_log, d_skip=d_skip, rms_w=rms_w, w_out=w_out, m1=m1, b1=b1, m2=m2, b2=b2,
                 w1=w1, s1=s1, w2=w2, s2=s2, h1=h1, sh1=sh1, h2=h2, sh2=sh2, w3=w3, s3=s3, cT=cT,
                 wmod=wmod, out=out)
        with ExitStack() as ctx:
            mamba(nc, ctx, sem, g)
        with ExitStack() as ctx:
            feed_forward(nc, ctx, sem, g)


def rows(v, n):
    return v.rearrange("(m p) -> p m", p=n)


def mamba(nc, ctx, sem, g):
    ident, ones, neg_half = g["ident"], g["ones"], g["neg_half"]
    mod_d, x1_d = g["mod_d"], g["x1_d"]
    s_fill, s_const = g["s_fill"], g["s_const"]

    def sb(name, shape, dt=F32):
        return ctx.enter_context(nc.sbuf_tensor(name, shape, dt))

    win = [sb(f"win{j}", [P, KD, ZX], F32R) for j in range(2)]
    wout = [sb(f"wout{j}", [P, QI, D], F32R) for j in range(2)]
    wm1 = [sb(f"wm1{j}", [P, KD, FF], F32R) for j in range(2)]
    wm2 = [sb(f"wm2{j}", [P, KF, D], F32R) for j in range(2)]
    wdt = sb("wdt", [P, KD, NH])
    lnw = sb("lnw", [P, KD])
    lnb = sb("lnb", [P, KD])
    cw = sb("cw", [P, XM, TAPS])
    cb = sb("cb", [P, XM])
    rmsw = sb("rmsw", [P, QI])
    b1c = sb("b1c", [P, KF])
    b2r = sb("b2r", [P, D])
    dtb = sb("dtb", [P, 1])
    nega = sb("nega", [P, 1])
    dsk = sb("dsk", [P, QI])
    tri = sb("tri", [P, P])
    pick = sb("pick", [96, QI, P], BF16)
    cleft = sb("cleft", [99, NC, P], BF16)
    cright = [sb(f"cright{j}", [99, NH, P], BF16) for j in range(2)]
    state = sb("state", [P, DI])
    cin = sb("cin", [P, XM, TAPS - 1 + HALF])
    xpad = [sb(f"xpad{j}", [P, NH // 2, 2, 2, HD]) for j in range(2)]

    us, ucs = range(NU), [(u, c) for u in range(NU) for c in range(NC)]
    groups = [(u, c, i) for u, c in ucs for i in range(NG)]
    banks = Handover(sem, "bank", list(mamba_bank_order()), 4)
    xin = Handover(sem, "x", list(us), 2, fills=16, uses=16)
    h_shsc = Handover(sem, "shsc", [0], 1, fills=16, both=False)
    h_gate = Handover(sem, "gate", [0], 1, fills=16, both=False)
    h_es = Handover(sem, "decay", groups, 2, both=False)
    h_mh = Handover(sem, "mh", groups, 2)
    h_right = Handover(sem, "cright", ucs, 2, fills=48, both=False)
    h_yoff = Handover(sem, "yoff", [k for k in ucs if k != (0, 0)], 1)
    h_ysum = Handover(sem, "yaddends", ucs, 1)
    h_yhl = Handover(sem, "yhalves", ucs, 1, both=False)
    h_eb = Handover(sem, "ebank", groups, 2)
    c_yin = Count(sem, "yin_made", NU * NC)
    c_stat = Count(sem, "variance_made", NU * (3 + NC))
    c_rstd = Count(sem, "rstd_made", NU * (3 + NC))
    c_norm = Count(sem, "norm_made", NU * 2)
    c_ah = Count(sem, "act_hi_made", NU * 2)
    c_al = Count(sem, "act_lo_made", NU * 2)
    c_cacc = Count(sem, "conv_made", NU * XM)
    c_xc = Count(sem, "xc_made", NU * XM)
    c_dexp = Count(sem, "dexp_made", NU)
    c_cum = Count(sem, "cum_parts_made", NU)
    c_wexp = Count(sem, "wexp_made", NU)
    c_wv = Count(sem, "wv_made", NU)
    c_left = Count(sem, "cleft_made", NU)
    c_yg = Count(sem, "y_gated", NU * NC)
    c_yh = Count(sem, "y_hi_made", NU * NC)
    c_ysq = Count(sem, "y_squared", NU * NC)
    c_hh = Count(sem, "hidden_hi_made", NU * KF)
    c_hl = Count(sem, "hidden_lo_made", NU * KF)
    c_o1 = Count(sem, "o1_biased", NU)
    c_x1 = Count(sem, "x1_made", NU)
    own_dve = Steps(sem, "dve_steps", DVE_STEPS)
    own_act = Steps(sem, "act_steps", 2 * NU)
    counts = [v for v in locals().values() if isinstance(v, (Handover, Count))]

    with ExitStack() as own:
        def tmp(name, shape, dt=F32):
            return own.enter_context(nc.sbuf_tensor(name, shape, dt))

        stage = tmp("stage", [P, KD * ZX])
        ct = tmp("ct", [P, KD, B])
        wm = tmp("wm", [P, KD, 6 * D])
        mod = tmp("mod", [B, 6 * D])
        ga_a = tmp("ga_a", [B, 2, D])
        mp = own.enter_context(nc.psum_tensor("mp", [B, 3, 512], F32))
        s_vec = sem("s_vec")
        s_small = sem("s_small")
        s_stage = sem("s_stage")
        s_split = sem("s_split")
        s_ct = sem("s_ct")
        s_silu = sem("s_silu")
        s_mod = sem("s_mod")
        s_modrow = sem("s_modrow")
        s_store = sem("s_store")
        s_copy = sem("s_copy")
        s_a = sem("s_a")
        splits = [(g["w_in"][:, 0:ZX].rearrange("(k p) n -> p k n", p=P), win, KD, ZX),
                  (g["w_out"].rearrange("(k p) n -> p k n", p=P), wout, QI, D),
                  (g["m1"].rearrange("(k p) n -> p k n", p=P), wm1, KD, FF),
                  (g["m2"].rearrange("(k p) n -> p k n", p=P), wm2, KF, D)]
        block = own.enter_context(nc.Block())

        @block.sync
        def _(sp):
            start(sp, counts)
            sp.dma_start(ct[:], g["cT"].rearrange("(k p) b -> p k b", p=P)).then_inc(s_ct, 16)
            sp.dma_start(wm[:], g["wmod"].rearrange("(k p) n -> p k n", p=P)).then_inc(s_ct, 16)
            for i, (src, _, k, n) in enumerate(splits):
                if i:
                    sp.wait_ge(s_split, 2 * i)
                sp.dma_start(stage[:, 0:k * n].rearrange("p (k n) -> p k n", k=k), src).then_inc(s_stage, 16)
            sp.wait_ge(s_modrow, 6)
            sp.dma_start(mod_d, mod[:]).then_inc(s_store, 16)
            for name, dst in zip(("w1", "w2", "h1", "h2", "w3"), g["ffn_d"]):
                k = dst.shape[1] // g[name].shape[1]
                sp.dma_start(dst.rearrange("p (k n) -> p k n", k=k),
                             g[name].rearrange("(k p) n -> p k n", p=P)).then_inc(s_copy, 16)
            sp.wait_ge(s_store, 16)
            sp.wait_ge(s_copy, 80)

        @block.scalar
        def _(act):
            vecs = [(lnw[:], rows(g["ln_w"], P)), (lnb[:], rows(g["ln_b"], P)),
                    (cw[:], g["conv_w"].rearrange("(m p) k -> p m k", p=P)), (cb[:], rows(g["conv_b"], P)),
                    (rmsw[:], rows(g["rms_w"], P)), (b1c[:], rows(g["b1"], P)),
                    (b2r[:], g["b2"].partition_broadcast(P)),
                    (wdt[:], g["w_in"][:, ZX:ZX + NH].rearrange("(k p) n -> p k n", p=P))]
            for c in range(NC):
                vecs.append((dtb[NH * c:NH * c + NH, :], rows(g["dt_bias"], NH)))
                vecs.append((nega[NH * c:NH * c + NH, :], rows(g["a_log"], NH)))
            for h in range(HQ):
                vecs.append((dsk[HD * h:HD * h + HD, :],
                             g["d_skip"].rearrange("(q h) -> h q", h=HQ)[h].partition_broadcast(HD)))
            with nc.allow_non_contiguous_dma(reason="a few small vectors"):
                for dst, src in vecs:
                    act.dma_start(dst, src).then_inc(s_vec, 16)
            act.wait_ge(s_ct, 32)
            nc.scalar.activation(ct[:], ct[:], ACT.Silu).then_inc(s_silu, 1)
            act.wait_ge(s_vec, 16 * len(vecs))
            nc.scalar.activation(nega[:], nega[:], ACT.Exp).then_inc(s_a, 1)

        @block.tensor
        def _(pe):
            pe.wait_ge(s_silu, 1)
            for j in range(3):
                for k in range(KD):
                    mm = pe.matmul(mp[:, j, :], ct[:, k, :], wm[:, k, j * 512:(j + 1) * 512],
                                   start=(k == 0), stop=(k == KD - 1))
            mm.then_inc(s_mod, 1)

        @block.vector
        def _(dve):
            dve.memset(ones[:], 1.0).then_inc(s_const, 1)
            dve.memset(neg_half[:], -0.5)
            dve.memset(cin[:], 0.0)
            for j in range(2):
                dve.memset(xpad[j][:], 0.0)
            dve.wait_ge(s_mod, 1)
            mod_p = mp[:, :, :].rearrange("b j n -> b (j n)")
            for j in (0, 3):
                dve.tensor_copy(mod[:, j * D:(j + 1) * D], mod_p[:, j * D:(j + 1) * D]).then_inc(s_modrow, 1)
            for j in (1, 4):
                dve.tensor_scalar(mod[:, j * D:(j + 1) * D], mod_p[:, j * D:(j + 1) * D], 1.0, None,
                                  ALU.add).then_inc(s_modrow, 1)
            for i, j in enumerate((2, 5)):
                gp = mod_p[:, j * D:(j + 1) * D]
                dve.tensor_scalar(ga_a[:, 0, :], gp, 0.0, 2.0, ALU.is_ge, ALU.mult).then_inc(s_small, 1)
                dve.tensor_scalar(ga_a[:, 1, :], gp, -1.0, None, ALU.mult).then_inc(s_small, 1)
                dve.wait_ge(s_small, 5 * i + 2)
                dve.tensor_scalar(ga_a[:, 0, :], ga_a[:, 0, :], 1.0, None, ALU.subtract).then_inc(s_small, 1)
                dve.tensor_tensor(ga_a[:, 1, :], gp, ga_a[:, 1, :], ALU.max).then_inc(s_small, 1)
                dve.wait_ge(s_small, 5 * i + 4)
                dve.tensor_scalar(ga_a[:, 1, :], ga_a[:, 1, :], 0.25, None, ALU.max).then_inc(s_small, 1)
                dve.wait_ge(s_small, 5 * i + 5)
                dve.tensor_tensor(mod[:, j * D:(j + 1) * D], ga_a[:, 0, :], ga_a[:, 1, :],
                                  ALU.mult).then_inc(s_modrow, 1)
                dve.wait_ge(s_modrow, 5 + i)
            dve.wait_ge(s_a, 1)
            dve.tensor_scalar(nega[:], nega[:], -1.0, None, ALU.mult)
            for i, (_, halves, k, n) in enumerate(splits):
                dve.wait_ge(s_stage, 16 * (i + 1))
                w = stage[:, 0:k * n].rearrange("p (k n) -> p k n", k=k)
                if i == 1:
                    dve.wait_ge(s_vec, 16)
                    for q in range(k):
                        last = dve.tensor_scalar(w[:, q, :], w[:, q, :], rmsw[:, q:q + 1], None, ALU.mult)
                    last.then_inc(s_const, 1)
                    dve.wait_ge(s_const, 2)
                dve.tensor_copy(halves[0][:], w).then_inc(s_split, 1)
                dve.wait_ge(s_split, 2 * i + 1)
                dve.tensor_tensor(halves[1][:], w, halves[0][:].bitcast(F32), ALU.subtract).then_inc(s_split, 1)

        @block.gpsimd
        def _(pool):
            pool.memset(ident[:], 0.0)
            pool.memset(tri[:], 1.0)
            pool.memset(pick[:], 0.0)
            pool.memset(cleft[:], 0.0)
            for j in range(2):
                last = pool.memset(cright[j][:], 0.0)
            last.then_inc(s_fill, 1)
            pool.wait_ge(s_fill, 1)
            pool.memset(cleft[96:99, :, :], 1.0).then_inc(s_fill, 1)
            pool.wait_ge(s_fill, 2)
            pool.affine_select(out=ident[:], in_=ident[:], compare_op=ALU.not_equal, fill=1.0, base=0,
                               pattern=[[-1, P]], channel_multiplier=1)
            pool.affine_select(out=tri[:], in_=tri[:], compare_op=ALU.is_ge, fill=0.0, base=0,
                               pattern=[[1, P]], channel_multiplier=-1).then_inc(s_fill, 1)
            pool.wait_ge(s_fill, 3)
            for j in range(3):
                v = pick[:].rearrange("k q (h d) -> k (q h) d", d=HD)
                pool.affine_select(out=v, in_=v, compare_op=ALU.not_equal, fill=1.0, base=-NH * j,
                                   pattern=[[-1, NH], [0, HD]], channel_multiplier=1)
                for r in range(2):
                    v = cright[r][0:96, :, :]
                    last = pool.affine_select(out=v, in_=v, compare_op=ALU.not_equal, fill=-1.0,
                                              base=-NH * j, pattern=[[-1, NH], [0, P]], channel_multiplier=1)
                last.then_inc(s_fill, 1)
                pool.wait_ge(s_fill, 4 + j)

    xs = [sb(f"xs{u}", [P, NC, D]) for u in range(NU)]
    shsc = sb("shsc", [P, 2, D])
    gate = sb("gate", [P, D])
    res = sb("res", [P, NC, D])
    nrm = sb("nrm", [P, NC, D])
    stats = sb("stats", [P, NC, 6])
    mv = sb("mv", [P, NC, 2])
    var = sb("var", [P, NC])
    rstd = sb("rstd", [P, NC])
    af = sb("af", [P, KD, HALF])
    ah = sb("ah", [P, KD, HALF], F32R)
    al = sb("al", [P, KD, HALF], F32R)
    dabs = sb("dabs", [P, P])
    dexp = dabs
    drelu = sb("drelu", [P, P])
    dden = sb("dden", [P, P])
    ds_ = sb("ds_", [P, P])
    dsq = sb("dsq", [P, P])
    dser = sb("dser", [P, P])
    dtv = sb("dtv", [P, P])
    da = dden
    cum = sb("cum", [P, P])
    crest = sb("crest", [P, 2, P])
    parts = sb("parts", [P, 3, P], BF16)
    wexp = sb("wexp", [P, P])
    wv = sb("wv", [P, P])
    cend = sb("cend", [P, 1])
    dend = sb("dend", [P, P])
    dtw = sb("dtw", [P, 2, NC, NH])
    dec = sb("dec", [P, NC, NH])
    xw = [sb(f"xw{j}", [P, DI]) for j in range(2)]
    bt = [sb(f"bt{j}", [P, P]) for j in range(2)]
    gm = [sb(f"gm{j}", [P, P]) for j in range(2)]
    es = [sb(f"es{j}", [P, G4, P]) for j in range(2)]
    mh = [sb(f"mh{j}", [P, G4, P]) for j in range(2)]
    yoff_s = sb("yoff_s", [P, QI, P])
    yin_s = sb("yin_s", [P, QI, P])
    yg = sb("yg", [P, QI, P])
    ysq = yoff_s
    ysum = sb("ysum", [P, P])
    yh = sb("yh", [P, QI, P], F32R)
    yl = sb("yl", [P, QI, P], F32R)
    ms = sb("ms", [P, 1])
    rms = sb("rms", [P, 1])
    hf = [sb(f"hf{j}", [P, HALF]) for j in range(2)]
    o1 = sb("o1", [P, NC, D])

    with ExitStack() as mixer:
        def mx(name, shape, dt=F32):
            return mixer.enter_context(nc.sbuf_tensor(name, shape, dt))

        sz = mx("sz", [P, QI, HALF])
        ec = mx("ec", [P, QI, HALF])
        xc = mx("xc", [P, XM, HALF])
        cacc = [mx(f"cacc{j}", [P, HALF]) for j in range(2)]
    hh = sb("hh", [P, KF, HALF], F32R)
    hl = sb("hl", [P, KF, HALF], F32R)

    with ExitStack() as own:
        bank = [own.enter_context(nc.psum_tensor(f"bank{j}", [P, 512], F32)) for j in range(4)]
        eb = [own.enter_context(nc.psum_tensor(f"eb{j}", [P, 512], F32)) for j in range(2)]
        yin = own.enter_context(nc.psum_tensor("yin", [P, QI, P], F32))
        yoff = own.enter_context(nc.psum_tensor("yoff", [P, QI, P], F32))

        block = own.enter_context(nc.Block())

        @block.sync
        def _(sp):
            with sp.Fori(0, B) as b:
                for u in us:
                    sp.wait_ge(xin.free(u), xin.used_before(b, u))
                    sp.dma_start(xs[u][:], g["x"][b, u * HALF:(u + 1) * HALF, :].rearrange(
                        "(c p) d -> p c d", p=P)).then_inc(xin.full(u), 16)
                    if u == 0:
                        sp.wait_ge(c_x1.sem, c_x1.at(b, 0))
                        sp.dma_start(shsc[:], mod_d[b, 0:2 * D].rearrange("(j d) -> j d", d=D)
                                     .partition_broadcast(P)).then_inc(h_shsc.full(0), 16)
                        sp.dma_start(gate[:], mod_d[b, 2 * D:3 * D].partition_broadcast(P)).then_inc(h_gate.full(0), 16)
                    sp.wait_ge(c_cum.sem, c_cum.at(b, u + 1))
                    for c in range(NC):
                        key = (u, c)
                        if c >= 2:
                            sp.wait_ge(h_mh.free((u, c - 2, NG - 1)), h_mh.used(b, (u, c - 2, NG - 1)))
                        for j in range(3):
                            sp.dma_start(cright[c % 2][96 + j:97 + j, :, :],
                                         parts[NH * c:NH * c + NH, j, :]).then_inc(h_right.full(key), 16)
                    sp.wait_ge(c_x1.sem, c_x1.at(b, u + 1))
                    sp.dma_start(x1_d[b, u * HALF:(u + 1) * HALF, :].rearrange("(c p) d -> p c d", p=P),
                                 xs[u][:]).then_inc(xin.free(u), 16)
            for u in us:
                sp.wait_ge(xin.free(u), 16 * B + START)

        @block.tensor
        def _(pe):
            def product(o, left, right, first=True, last=True):
                for n, (a, c) in enumerate(((0, 0), (0, 1), (1, 0))):
                    mm = pe.matmul(o, left[a], right[c], start=(first and n == 0), stop=(last and n == 2))
                return mm

            with pe.Fori(0, B) as b:
                for u in us:
                    def transposed(which, name):
                        pe.wait_ge(c_norm.sem, c_norm.at(b, 2 * u + (which == "m") + 1))
                        for k in range(KD):
                            key = (u, name, k)
                            pe.wait_ge(banks.free(key), banks.used_before(b, key))
                            for c in range(NC):
                                mm = pe.transpose(bank[banks.slot(key)][:, c * P:(c + 1) * P],
                                                  nrm[:, c, k * P:(k + 1) * P], ident[:])
                            mm.then_inc(banks.full(key), 1)

                    transposed("a", "nT")
                    key = (u, "dt")
                    for k in range(KD):
                        pe.wait_ge(banks.free((u, "nT", k)), banks.used(b, (u, "nT", k)))
                    pe.wait_ge(banks.free(key), banks.used_before(b, key))
                    for c in range(NC):
                        for k in range(KD):
                            mm = pe.matmul(bank[banks.slot(key)][NH * c:NH * c + NH, 0:P], wdt[:, k, :],
                                           af[:, k, c * P:(c + 1) * P], start=(k == 0), stop=(k == KD - 1),
                                           tile_position=(0, NH * c))
                    mm.then_inc(banks.full(key), 1)
                    pe.wait_ge(c_al.sem, c_al.at(b, 2 * u + 1))
                    for m in PROJ:
                        key = (u, "in", m)
                        pe.wait_ge(banks.free(key), banks.used_before(b, key))
                        for k in range(KD):
                            mm = product(bank[banks.slot(key)][:], [w[:, k, m * P:(m + 1) * P] for w in win],
                                         [a[:, k, :] for a in (ah, al)], k == 0, k == KD - 1)
                        mm.then_inc(banks.full(key), 1)

                    key = (u, "dtw")
                    pe.wait_ge(c_wv.sem, c_wv.at(b, u + 1))
                    pe.wait_ge(banks.free(key), banks.used_before(b, key))
                    pe.transpose(bank[banks.slot(key)][:, 0:P], dtv[:], ident[:])
                    pe.transpose(bank[banks.slot(key)][:, P:2 * P], wv[:], ident[:]).then_inc(banks.full(key), 1)
                    key = (u, "dec")
                    pe.wait_ge(banks.free(key), banks.used_before(b, key))
                    pe.matmul(bank[banks.slot(key)][:, 0:P], ones[:], dend[:], start=True, stop=True)\
                        .then_inc(banks.full(key), 1)
                    pe.wait_ge(c_left.sem, c_left.at(b, u + 1))
                    for q in range(QI):
                        key = (u, "ec", q)
                        pe.wait_ge(banks.free(key), banks.used_before(b, key))
                        pe.matmul(bank[banks.slot(key)][:], pick[:, q, :],
                                  cleft[0:96, :, :].rearrange("k c t -> k (c t)"), start=True, stop=True)\
                            .then_inc(banks.full(key), 1)

                    def by_token(c):
                        key = (u, "xT", c)
                        pe.wait_ge(banks.free(key), banks.used_before(b, key))
                        for q in range(QI):
                            mm = pe.transpose(bank[banks.slot(key)][:, q * P:(q + 1) * P],
                                              xc[:, q, c * P:(c + 1) * P], ident[:])
                        mm.then_inc(banks.full(key), 1)
                        key = (u, "bt", c)
                        pe.wait_ge(banks.free(key), banks.used_before(b, key))
                        pe.transpose(bank[banks.slot(key)][:, 0:P], xc[:, QI, c * P:(c + 1) * P], ident[:])
                        pe.matmul(bank[banks.slot(key)][:, P:2 * P], xc[:, QI, c * P:(c + 1) * P],
                                  xc[:, QI + 1, c * P:(c + 1) * P], start=True, stop=True)\
                            .then_inc(banks.full(key), 1)

                    def decay(c, i):
                        key = (u, c, i)
                        pe.wait_ge(h_eb.free(key), h_eb.used_before(b, key))
                        mm = pe.matmul(eb[i % 2][:], cleft[:, c, :],
                                       cright[c % 2][:, G4 * i:G4 * (i + 1), :].rearrange("k h t -> k (h t)"),
                                       start=True, stop=True)
                        mm.then_inc(h_eb.full(key), 1)

                    def intra(c, i):
                        key = (u, c, i)
                        pe.wait_ge(h_mh.full(key), h_mh.filled(b, key))
                        for j in range(G4):
                            h = G4 * i + j
                            row = HD * 2 * (h % HQ // 2)
                            mm = pe.matmul(yin[row:row + 2 * HD, h // HQ, :],
                                           xpad[c % 2][:, h // 2, h % 2, :, :].rearrange("s w d -> s (w d)"),
                                           mh[i % 2][:, j, :], start=(h % 2 == 0), stop=(h % 2 == 1),
                                           tile_position=(0, row))
                        mm.then_inc(h_mh.free(key), 1)

                    def from_state(c):
                        last = (u, "st", c - 1) if c else (u - 1, "st", NC - 1)
                        pe.wait_ge(banks.free(last), banks.used(b, last))
                        pe.wait_ge(h_yoff.free((u, c)), h_yoff.used_before(b, (u, c)))
                        for q in range(QI):
                            mm = pe.matmul(yoff[:, q, :], state[:, q * P:(q + 1) * P],
                                           xc[:, QI + 1, c * P:(c + 1) * P], start=True, stop=True)
                        mm.then_inc(h_yoff.full((u, c)), 1)

                    def project(c):
                        key = (u, "op", c)
                        pe.wait_ge(h_yhl.full((u, c)), h_yhl.filled(b, (u, c)))
                        pe.wait_ge(banks.free(key), banks.used_before(b, key))
                        pe.matmul(bank[banks.slot(key)][:, D:D + 1], ysum[:], ones[:, 0:1], start=True, stop=True)
                        for q in range(QI):
                            mm = product(bank[banks.slot(key)][:, 0:D], [y[:, q, :] for y in (yh, yl)],
                                         [w[:, q, :] for w in wout], q == 0, q == QI - 1)
                        mm.then_inc(banks.full(key), 1)

                    pe.wait_ge(c_xc.sem, c_xc.at(b, XM * (u + 1)))
                    by_token(0)
                    for c in range(NC):
                        pe.wait_ge(h_right.full((u, c)), h_right.filled(b, (u, c)))
                        pe.wait_ge(banks.free((u, "bt", c)), banks.used(b, (u, "bt", c)))
                        for i in range(NG):
                            decay(c, i)
                            if i == 1:
                                pe.wait_ge(h_ysum.full((u, c)), h_ysum.filled_before(b, (u, c)))
                            if i:
                                intra(c, i - 1)
                            if i == 2 and (u, c) != (0, 0):
                                from_state(c)
                            if i == 3 and c + 1 < NC:
                                by_token(c + 1)
                        intra(c, NG - 1)
                        key = (u, "st", c)
                        pe.wait_ge(banks.free(key), banks.used_before(b, key))
                        pe.matmul(bank[banks.slot(key)][:], bt[c % 2][:], xw[c % 2][:], start=True, stop=True)\
                            .then_inc(banks.full(key), 1)
                        if c:
                            project(c - 1)
                    project(NC - 1)

                    transposed("m", "mT")
                    pe.wait_ge(c_al.sem, c_al.at(b, 2 * u + 2))
                    for m in range(KF):
                        key = (u, "m1", m)
                        pe.wait_ge(banks.free(key), banks.used_before(b, key))
                        for k in range(KD):
                            mm = product(bank[banks.slot(key)][:], [w[:, k, m * P:(m + 1) * P] for w in wm1],
                                         [a[:, k, :] for a in (ah, al)], k == 0, k == KD - 1)
                        mm.then_inc(banks.full(key), 1)
                    for j in range(NC // 2):
                        key = (u, "m2", j)
                        pe.wait_ge(banks.free(key), banks.used_before(b, key))
                        for c in range(2 * j, 2 * j + 2):
                            for k in range(KF):
                                if c == 0:
                                    pe.wait_ge(c_hl.sem, c_hl.at(b, KF * u + k + 1))
                                mm = product(bank[banks.slot(key)][:, (c % 2) * D:(c % 2 + 1) * D],
                                             [h[:, k, c * P:(c + 1) * P] for h in (hh, hl)],
                                             [w[:, k, :] for w in wm2], k == 0, k == KF - 1)
                        mm.then_inc(banks.full(key), 1)

        @block.scalar
        def _(act):
            with act.Fori(0, B) as b:
                for u in us:
                    def affine(name):
                        for k in range(KD):
                            key = (u, name, k)
                            act.wait_ge(banks.full(key), banks.filled(b, key))
                            nc.scalar.activation(af[:, k, :], bank[banks.slot(key)][:], ACT.Identity,
                                                 bias=lnb[:, k:k + 1], scale=lnw[:, k:k + 1])\
                                .then_inc(banks.free(key), 1)

                    affine("nT")
                    key = (u, "dt")
                    act.wait_ge(banks.full(key), banks.filled(b, key))
                    n = own_act.mark(nc.scalar.activation(dabs[:], bank[banks.slot(key)][:, 0:P], ACT.Abs,
                                                          bias=dtb[:]))
                    nc.scalar.activation(drelu[:], bank[banks.slot(key)][:, 0:P], ACT.Relu, bias=dtb[:])\
                        .then_inc(banks.free(key), 1)
                    act.wait_ge(own_act.sem, own_act.at(b, n))
                    nc.scalar.activation(dexp[:], dabs[:], ACT.Exp, scale=-1.0).then_inc(c_dexp.sem, 1)
                    for m in PROJ[:XM]:
                        key = (u, "in", m)
                        act.wait_ge(banks.full(key), banks.filled(b, key))
                        nc.scalar.activation(cin[:, m - QI, TAPS - 1:], bank[banks.slot(key)][:], ACT.Copy)\
                            .then_inc(banks.free(key), 1)
                    act.wait_ge(c_cum.sem, c_cum.at(b, u + 1))
                    own_n = own_act.mark(nc.scalar.activation(cend[:], cum[:, P - 1:P], ACT.Exp))
                    nc.scalar.activation(wexp[:], cum[:], ACT.Exp, bias=cum[:, P - 1:P], scale=-1.0)\
                        .then_inc(c_wexp.sem, 1)
                    for m in PROJ[XM:]:
                        key = (u, "in", m)
                        act.wait_ge(banks.full(key), banks.filled(b, key))
                        nc.scalar.activation(sz[:, m, :], bank[banks.slot(key)][:], ACT.Silu)\
                            .then_inc(banks.free(key), 1)
                    for m in range(XM):
                        act.wait_ge(c_cacc.sem, c_cacc.at(b, XM * u + m + 1))
                        nc.scalar.activation(xc[:, m, :], cacc[m % 2][:], ACT.Silu).then_inc(c_xc.sem, 1)
                    for q in range(QI):
                        key = (u, "ec", q)
                        act.wait_ge(banks.full(key), banks.filled(b, key))
                        nc.scalar.activation(ec[:, q, :], bank[banks.slot(key)][:], ACT.Exp)\
                            .then_inc(banks.free(key), 1)

                    def y_out(c):
                        act.wait_ge(c_yg.sem, c_yg.at(b, NC * u + c + 1))
                        last = (u, "op", c - 1) if c else None
                        if last:
                            act.wait_ge(banks.full(last), banks.filled(b, last))
                        nc.scalar.activation(yh[:], yg[:], ACT.Copy).then_inc(c_yh.sem, 1)
                        nc.scalar.activation(ysq[:], yg[:], ACT.Square).then_inc(c_ysq.sem, 1)

                    for c in range(NC):
                        for i in range(NG):
                            key = (u, c, i)
                            act.wait_ge(h_eb.full(key), h_eb.filled(b, key))
                            act.wait_ge(h_mh.full(key), h_mh.filled_before(b, key))
                            e = es[i % 2][:].rearrange("s h t -> s (h t)")
                            nc.scalar.activation(e, eb[i % 2][:], ACT.Relu, scale=-1.0).then_inc(h_eb.free(key), 1)
                            act.wait_ge(h_eb.free(key), h_eb.used(b, key))
                            nc.scalar.activation(e, e, ACT.Exp, scale=-1.0).then_inc(h_es.full(key), 1)
                            if i == 5 and c:
                                y_out(c - 1)
                    y_out(NC - 1)

                    affine("mT")
                    for m in range(KF):
                        key = (u, "m1", m)
                        act.wait_ge(banks.full(key), banks.filled(b, key))
                        if m >= 2:
                            act.wait_ge(c_hl.sem, c_hl.at(b, KF * u + m - 1))
                        nc.scalar.activation(hf[m % 2][:], bank[banks.slot(key)][:], ACT.Relu,
                                             bias=b1c[:, m:m + 1]).then_inc(banks.free(key), 1)
            own_act.closed()

        @block.gpsimd
        def _(pool):
            with pool.Fori(0, B) as b:
                for u in us:
                    turn = [0]

                    def power(t, v, n):
                        at = (3 + NC) * u + turn[0] + 1
                        turn[0] += 1
                        pool.wait_ge(c_stat.sem, c_stat.at(b, at))
                        pool.tensor_tensor(t, v, neg_half[:, 0:n], ALU.pow).then_inc(c_rstd.sem, 1)

                    def high(name, k0):
                        for k in range(KD):
                            pool.wait_ge(banks.free((u, name, k)), banks.used(b, (u, name, k)))
                        pool.sem_inc(s_fill, 1)
                        pool.tensor_scalar(ah[:], af[:], 1.0, 0.0, ALU.mult, ALU.add).then_inc(c_ah.sem, 1)

                    power(rstd[:], var[:], NC)
                    power(rstd[:], var[:], NC)
                    high("nT", 0)
                    pool.wait_ge(c_cum.sem, c_cum.at(b, u + 1))
                    pool.sem_inc(s_fill, 1)
                    for c in range(NC):
                        for j in range(3):
                            last = pool.tensor_copy(cleft[NH * j:NH * (j + 1), c, :],
                                                    parts[NH * c:NH * (c + 1), j, :])
                    last.then_inc(c_left.sem, 1)
                    for c in range(NC):
                        key = (u, c)
                        pool.wait_ge(h_ysum.full(key), h_ysum.filled(b, key))
                        if c:
                            pool.wait_ge(h_yhl.full((u, c - 1)), h_yhl.filled(b, (u, c - 1)))
                        if (u, c) != (0, 0):
                            pool.tensor_tensor(yg[:], yin_s[:], yoff_s[:], ALU.add).then_inc(h_ysum.free(key), 1)
                            pool.wait_ge(h_ysum.free(key), h_ysum.used(b, key))
                            pool.tensor_tensor(yg[:], yg[:], sz[:, :, c * P:(c + 1) * P], ALU.mult)\
                                .then_inc(c_yg.sem, 1)
                        else:
                            pool.sem_inc(s_fill, 1)
                            pool.tensor_copy(yg[:], yin_s[:]).then_inc(h_ysum.free(key), 1)
                            pool.wait_ge(h_ysum.free(key), h_ysum.used(b, key))
                            pool.tensor_tensor(yg[:], yg[:], sz[:, :, c * P:(c + 1) * P], ALU.mult)\
                                .then_inc(c_yg.sem, 1)
                        if c:
                            power(rms[:], ms[:], 1)
                    power(rms[:], ms[:], 1)
                    power(rstd[:], var[:], NC)
                    pool.wait_ge(c_norm.sem, c_norm.at(b, 2 * u + 2))
                    for c in range(NC):
                        last = pool.tensor_tensor(o1[:, c, :], o1[:, c, :], b2r[:], ALU.add)
                    last.then_inc(c_o1.sem, 1)
                    high("mT", 0)
                    for m in range(KF):
                        pool.wait_ge(banks.free((u, "m1", m)), banks.used(b, (u, "m1", m)))
                        pool.sem_inc(s_fill, 1)
                        pool.tensor_scalar(hh[:, m, :], hf[m % 2][:], 1.0, 0.0, ALU.mult, ALU.add)\
                            .then_inc(c_hh.sem, 1)

        @block.vector
        def _(dve):
            with dve.Fori(0, B) as b:
                def mark(ins):
                    return own_dve.mark(ins)

                def after(n):
                    dve.wait_ge(own_dve.sem, own_dve.at(b, n))

                for u in us:
                    turn = [0]

                    def powered():
                        turn[0] += 1
                        dve.wait_ge(c_rstd.sem, c_rstd.at(b, (3 + NC) * u + turn[0]))

                    def normalise(dst, src):
                        for c in range(NC):
                            n = mark(dve.bn_stats(stats[:, c, :], src[:, c, :])) if c == NC - 1 else \
                                dve.bn_stats(stats[:, c, :], src[:, c, :])
                        after(n)
                        dve.sem_inc(s_const, 1)
                        for c in range(NC):
                            last = dve.bn_aggr(mv[:, c, :], stats[:, c, :])
                        after(mark(last))
                        dve.tensor_scalar(var[:], mv[:, :, 1], EPS, None, ALU.add).then_inc(c_stat.sem, 1)
                        powered()
                        for c in range(NC):
                            last = dve.tensor_scalar(dst[:, c, :], src[:, c, :], mv[:, c, 0:1], rstd[:, c:c + 1],
                                                     ALU.subtract, ALU.mult)
                        return last

                    def low(name, i):
                        for k in range(KD):
                            dve.wait_ge(banks.free((u, name, k)), banks.used(b, (u, name, k)))
                        dve.wait_ge(c_ah.sem, c_ah.at(b, 2 * u + i + 1))
                        dve.tensor_tensor(al[:], af[:], ah[:].bitcast(F32), ALU.subtract).then_inc(c_al.sem, 1)

                    dve.wait_ge(xin.full(u), xin.filled(b, u))
                    after(mark(normalise(res, xs[u])))
                    if u == 0:
                        dve.wait_ge(h_shsc.full(0), h_shsc.filled(b, 0))
                    after(mark(dve.tensor_tensor(res[:], res[:], shsc[:, 1:2, :].to_broadcast([P, NC, D]), ALU.mult)))
                    after(mark(dve.tensor_tensor(res[:], res[:], shsc[:, 0:1, :].to_broadcast([P, NC, D]), ALU.add)))
                    normalise(nrm, res).then_inc(c_norm.sem, 1)
                    low("nT", 0)

                    dve.wait_ge(c_dexp.sem, c_dexp.at(b, u + 1))
                    after(mark(dve.tensor_scalar(dden[:], dexp[:], 2.0, None, ALU.add)))
                    after(mark(dve.reciprocal(dden[:], dden[:])))
                    after(mark(dve.tensor_tensor(ds_[:], dexp[:], dden[:], ALU.mult)))
                    after(mark(dve.tensor_tensor(dsq[:], ds_[:], ds_[:], ALU.mult)))
                    after(mark(dve.tensor_scalar(dser[:], dsq[:], 1.0 / (2 * SERIES + 1), None, ALU.mult)))
                    for i in range(SERIES - 1, 0, -1):
                        after(mark(dve.scalar_tensor_tensor(out=dser[:], in0=dser[:], scalar=1.0 / (2 * i + 1),
                                                            in1=dsq[:], op0=ALU.add, op1=ALU.mult)))
                    after(mark(dve.scalar_tensor_tensor(out=dser[:], in0=dser[:], scalar=1.0, in1=ds_[:],
                                                        op0=ALU.add, op1=ALU.mult)))
                    after(mark(dve.scalar_tensor_tensor(out=dtv[:], in0=dser[:], scalar=2.0, in1=drelu[:],
                                                        op0=ALU.mult, op1=ALU.add)))
                    after(mark(dve.tensor_scalar(da[:], dtv[:], nega[:], None, ALU.mult)))
                    after(mark(dve.tensor_tensor_scan(cum[:], ones[:], da[:], 0.0, ALU.mult, ALU.add)))
                    after(mark(dve.tensor_copy(parts[:, 0, :], cum[:])))
                    after(mark(dve.tensor_tensor(crest[:, 0, :], cum[:], parts[:, 0, :], ALU.subtract)))
                    after(mark(dve.tensor_copy(parts[:, 1, :], crest[:, 0, :])))
                    after(mark(dve.tensor_tensor(crest[:, 1, :], crest[:, 0, :], parts[:, 1, :], ALU.subtract)))
                    dve.tensor_copy(parts[:, 2, :], crest[:, 1, :]).then_inc(c_cum.sem, 1)
                    dve.wait_ge(c_wexp.sem, c_wexp.at(b, u + 1))
                    mark(dve.tensor_scalar(dend[:], ident[:], cend[:], None, ALU.mult))
                    dve.tensor_tensor(wv[:], wexp[:], dtv[:], ALU.mult).then_inc(c_wv.sem, 1)

                    for m in range(XM):
                        key = (u, "in", QI + m)
                        dve.wait_ge(banks.free(key), banks.used(b, key))
                        if m >= 2:
                            dve.wait_ge(c_xc.sem, c_xc.at(b, XM * u + m - 1))
                        n = mark(dve.tensor_scalar(cacc[m % 2][:], cin[:, m, 0:HALF], cw[:, m, 0:1], cb[:, m:m + 1],
                                                   ALU.mult, ALU.add))
                        for t in range(1, TAPS):
                            after(n)
                            ins = dve.scalar_tensor_tensor(
                                out=cacc[m % 2][:], in0=cin[:, m, t:t + HALF], scalar=cw[:, m, t:t + 1],
                                in1=cacc[m % 2][:], op0=ALU.mult, op1=ALU.add)
                            if t < TAPS - 1:
                                n = mark(ins)
                            else:
                                ins.then_inc(c_cacc.sem, 1)
                        dve.wait_ge(c_cacc.sem, c_cacc.at(b, XM * u + m + 1))
                        tail = cin[:, m, 0:TAPS - 1]
                        last = dve.tensor_copy(tail, cin[:, m, HALF:]) if u < NU - 1 else dve.memset(tail, 0.0)
                    n_tail = mark(last)

                    key = (u, "dtw")
                    dve.wait_ge(banks.full(key), banks.filled(b, key))
                    dve.tensor_copy(dtw[:].rearrange("s w c h -> s (w c h)"), bank[banks.slot(key)][:, 0:2 * P])\
                        .then_inc(banks.free(key), 1)
                    dve.wait_ge(banks.free(key), banks.used(b, key))
                    key = (u, "dec")
                    dve.wait_ge(banks.full(key), banks.filled(b, key))
                    dve.tensor_copy(dec[:].rearrange("n c h -> n (c h)"), bank[banks.slot(key)][:, 0:P])\
                        .then_inc(banks.free(key), 1)

                    def by_token(c):
                        key = (u, "xT", c)
                        dve.wait_ge(banks.full(key), banks.filled(b, key))
                        xt = bank[banks.slot(key)][:].rearrange("s (h d) -> s h d", d=HD)
                        for w in range(2):
                            dve.tensor_tensor(xpad[c % 2][:, :, w, w, :],
                                              xt.rearrange("s (h w) d -> s h w d", w=2)[:, :, w, :],
                                              dtw[:, 0, c, w::2].unsqueeze(2).to_broadcast([P, NH // 2, HD]), ALU.mult)
                        dve.tensor_tensor(xw[c % 2][:].rearrange("s (h d) -> s h d", d=HD), xt,
                                          dtw[:, 1, c, :].unsqueeze(2).to_broadcast([P, NH, HD]), ALU.mult)\
                            .then_inc(banks.free(key), 1)
                        key = (u, "bt", c)
                        dve.wait_ge(banks.full(key), banks.filled(b, key))
                        dve.tensor_copy(bt[c % 2][:], bank[banks.slot(key)][:, 0:P])
                        dve.tensor_tensor(gm[c % 2][:], bank[banks.slot(key)][:, P:2 * P], tri[:], ALU.mult)\
                            .then_inc(banks.free(key), 1)

                    def addends(c):
                        key, t = (u, c), slice(c * P, (c + 1) * P)
                        dve.wait_ge(h_ysum.free(key), h_ysum.used_before(b, key))
                        if key != (0, 0):
                            dve.wait_ge(h_yoff.full(key), h_yoff.filled(b, key))
                            for q in range(QI):
                                dve.wait_ge(banks.free((u, "ec", q)), banks.used(b, (u, "ec", q)))
                            dve.tensor_tensor(yoff_s[:], yoff[:], ec[:, :, t], ALU.mult).then_inc(h_yoff.free(key), 1)
                        last = (u, c, NG - 1)
                        dve.wait_ge(h_mh.free(last), h_mh.used(b, last))
                        for q in range(QI):
                            ins = dve.scalar_tensor_tensor(out=yin_s[:, q, :], in0=xc[:, q, t], scalar=dsk[:, q:q + 1],
                                                           in1=yin[:, q, :], op0=ALU.mult, op1=ALU.add)
                        ins.then_inc(h_ysum.full(key), 1)

                    def y_halves(c):
                        key = (u, c)
                        dve.wait_ge(c_ysq.sem, c_ysq.at(b, NC * u + c + 1))
                        dve.tensor_reduce(ysum[:], ysq[:].rearrange("d q t -> d t q"), AX.X, ALU.add)
                        dve.tensor_tensor(yl[:], yg[:], yh[:].bitcast(F32), ALU.subtract).then_inc(h_yhl.full(key), 1)

                    def residual(c):
                        key = (u, "op", c)
                        dve.wait_ge(banks.full(key), banks.filled(b, key))
                        dve.tensor_scalar(ms[:], bank[banks.slot(key)][:, D:D + 1], 1.0 / DI, EPS,
                                          ALU.mult, ALU.add).then_inc(c_stat.sem, 1)
                        powered()
                        dve.scalar_tensor_tensor(out=o1[:, c, :], in0=bank[banks.slot(key)][:, 0:D], scalar=rms[:],
                                                 in1=res[:, c, :], op0=ALU.mult, op1=ALU.add)\
                            .then_inc(banks.free(key), 1)

                    by_token(0)
                    for c in range(NC):
                        dve.wait_ge(banks.free((u, "bt", c)), banks.used(b, (u, "bt", c)))
                        for i in range(NG):
                            key = (u, c, i)
                            dve.wait_ge(h_es.full(key), h_es.filled(b, key))
                            dve.wait_ge(h_mh.free(key), h_mh.used_before(b, key))
                            dve.tensor_tensor(mh[i % 2][:], es[i % 2][:],
                                              gm[c % 2][:].unsqueeze(1).to_broadcast([P, G4, P]),
                                              ALU.mult).then_inc(h_mh.full(key), 1)
                            if i == 1 and c:
                                addends(c - 1)
                                if c >= 2:
                                    residual(c - 2)
                            if i == 4 and c + 1 < NC:
                                by_token(c + 1)
                            if i == 6 and c:
                                y_halves(c - 1)
                        key = (u, "st", c)
                        first = (u, c) == (0, 0)
                        dve.wait_ge(banks.full(key), banks.filled(b, key))
                        if first:
                            dve.tensor_copy(state[:], bank[banks.slot(key)][:]).then_inc(banks.free(key), 1)
                        else:
                            s3 = state[:].rearrange("n (h d) -> n h d", d=HD)
                            dve.wait_ge(banks.free((u, "dec")), banks.used(b, (u, "dec")))
                            after(mark(dve.tensor_tensor(s3, s3, dec[:, c, :].unsqueeze(2).to_broadcast([P, NH, HD]),
                                                         ALU.mult)))
                            dve.tensor_tensor(state[:], state[:], bank[banks.slot(key)][:], ALU.add)\
                                .then_inc(banks.free(key), 1)
                        dve.wait_ge(banks.free(key), banks.used(b, key))
                    addends(NC - 1)
                    residual(NC - 2)
                    y_halves(NC - 1)
                    residual(NC - 1)

                    dve.wait_ge(banks.free((u, "op", NC - 1)), banks.used(b, (u, "op", NC - 1)))
                    normalise(nrm, o1).then_inc(c_norm.sem, 1)
                    low("mT", 1)
                    for m in range(KF):
                        dve.wait_ge(c_hh.sem, c_hh.at(b, KF * u + m + 1))
                        dve.tensor_tensor(hl[:, m, :], hf[m % 2][:], hh[:, m, :].bitcast(F32), ALU.subtract)\
                            .then_inc(c_hl.sem, 1)
                    dve.wait_ge(c_o1.sem, c_o1.at(b, u + 1))
                    if u == 0:
                        dve.wait_ge(h_gate.full(0), h_gate.filled(b, 0))
                    for j in range(NC // 2):
                        key, cc = (u, "m2", j), slice(2 * j, 2 * j + 2)
                        dve.wait_ge(banks.full(key), banks.filled(b, key))
                        dve.tensor_tensor(o1[:, cc, :], o1[:, cc, :],
                                          bank[banks.slot(key)][:].rearrange("p (c d) -> p c d", c=2), ALU.add)\
                            .then_inc(banks.free(key), 1)
                        dve.wait_ge(banks.free(key), banks.used(b, key))
                    after(mark(dve.tensor_tensor(o1[:], o1[:], gate[:].unsqueeze(1).to_broadcast([P, NC, D]),
                                                 ALU.mult)))
                    dve.tensor_tensor(xs[u][:], xs[u][:], o1[:], ALU.add).then_inc(c_x1.sem, 1)
            own_dve.closed()


FFN_BANKS = 6


def after_block(b, u):
    return (b, u + 1) if u < NU - 1 else (b + 1, 0)


def feed_forward(nc, ctx, sem, g):
    ident, ones, neg_half = g["ident"], g["ones"], g["neg_half"]
    mod_d, x1_d = g["mod_d"], g["x1_d"]
    s_fill, s_const = g["s_fill"], g["s_const"]

    def sb(name, shape, dt=F32):
        return ctx.enter_context(nc.sbuf_tensor(name, shape, dt))

    shapes = ((KD, FF), (KD, FF), (KF, FF), (KF, FF), (KF, D))
    ws = [sb(f"fw{i}", [P, k, n], F32R) for i, (k, n) in enumerate(shapes)]
    s1 = sb("s1", [P, KF])
    s2 = sb("s2", [P, KF])
    sh1 = sb("sh1", [P, KF])
    sh2 = sb("sh2", [P, KF])
    s3r = sb("s3r", [P, D])
    inexact = sb("inexact", [1, 1], I32)
    fx = [sb(f"fx{u}", [P, NC, D]) for u in range(NU)]
    csc = sb("csc", [P, KD])
    csh = sb("csh", [P, KD])
    gb = sb("gb", [P, D])
    stats = sb("fstats", [P, NC, 6])
    mv = sb("fmv", [P, NC, 2])
    var = sb("fvar", [P, NC])
    rstd = sb("frstd", [P, NC])

    us = range(NU)
    layers = ("g", "h1", "h2")
    banks = Handover(sem, "fbank", list(ffn_bank_order()), FFN_BANKS)
    fronts = Handover(sem, "front", [(u, k) for u in us for k in range(KD)], KD)
    xin = Handover(sem, "fx", list(us), 2, fills=16, uses=16)
    c_mod = Count(sem, "fmod_loaded", 32)
    c_gbin = Count(sem, "gb_loaded", 16)
    c_stat = Count(sem, "fvariance_made", NU)
    c_rstd = Count(sem, "frstd_made", NU)
    c_norm = Count(sem, "fnorm_made", NU)
    c_ah = Count(sem, "fact_hi_made", NU)
    c_al = Count(sem, "fact_lo_made", NU)
    c_hi = Count(sem, "fhidden_hi_made", NU * 3 * KF)
    c_lo = Count(sem, "fhidden_lo_made", NU * 3 * KF)
    c_gb = Count(sem, "gb_made", 1)
    c_out = Count(sem, "out_made", NU)
    c_bn = Count(sem, "fstats_made", 2 * NU)
    s_passed = sem("fpassed")
    counts = [v for v in locals().values() if isinstance(v, (Handover, Count))]

    with ExitStack() as own:
        PIECE = 2048
        rounded = [own.enter_context(nc.sbuf_tensor(f"rounded{j}", [P, PIECE], F32R)) for j in range(2)]
        differs = own.enter_context(nc.sbuf_tensor("differs", [P, PIECE], F32))
        pieces = [(i, o, min(PIECE, k * n - o)) for i, (k, n) in enumerate(shapes) for o in range(0, k * n, PIECE)]
        count = own.enter_context(nc.sbuf_tensor("count", [P, len(pieces)], F32))
        total = own.enter_context(nc.sbuf_tensor("total", [P, 1], F32))
        sum_p = own.enter_context(nc.psum_tensor("sum_p", [1, 1], F32))
        s_w = [sem(f"s_ffn_w{i}") for i in range(len(shapes))]
        s_vec = sem("s_ffn_vec")
        s_round = sem("s_rounded")
        s_count = sem("s_counted")
        s_sum = sem("s_summed")
        s_flag = sem("s_flag")
        block = own.enter_context(nc.Block())

        @block.sync
        def _(sp):
            for i, w in enumerate(ws):
                sp.dma_start(w[:].rearrange("p k n -> p (k n)").bitcast(F32), g["ffn_d"][i]).then_inc(s_w[i], 16)
            start(sp, counts)
            with nc.allow_non_contiguous_dma(reason="a few small vectors"):
                for dst, name in ((s1, "s1"), (s2, "s2"), (sh1, "sh1"), (sh2, "sh2")):
                    sp.dma_start(dst[:], rows(g[name], P)).then_inc(s_vec, 16)
            sp.dma_start(s3r[:], g["s3"].partition_broadcast(P)).then_inc(s_vec, 16)
            sp.wait_ge(s_vec, 80)

        @block.vector
        def _(dve):
            for n, (i, o, size) in enumerate(pieces):
                if o == 0:
                    dve.wait_ge(s_w[i], 16)
                w = ws[i][:].rearrange("p k n -> p (k n)").bitcast(F32)[:, o:o + size]
                dve.tensor_copy(rounded[n % 2][:, 0:size], w).then_inc(s_round, 1)
                dve.wait_ge(s_round, n + 1)
                dve.scalar_tensor_tensor(out=differs[:, 0:size], in0=w, scalar=0.0,
                                         in1=rounded[n % 2][:, 0:size].bitcast(F32), op0=ALU.add,
                                         op1=ALU.not_equal, accum_out=count[:, n:n + 1]).then_inc(s_count, 1)
            dve.wait_ge(s_count, len(pieces))
            dve.tensor_reduce(total[:], count[:], AX.X, ALU.add).then_inc(s_count, 1)
            dve.wait_ge(s_sum, 1)
            dve.tensor_copy(inexact[:], sum_p[:]).then_inc(s_flag, 1)

        @block.tensor
        def _(pe):
            pe.wait_ge(s_count, len(pieces) + 1)
            pe.matmul(sum_p[:], total[:], ones[:, 0:1], start=True, stop=True).then_inc(s_sum, 1)

    nrm = sb("fnrm", [P, NC, D])
    go = sb("go", [P, NC, D])
    af = sb("faf", [P, KD, HALF])
    ah = sb("fah", [P, KD, HALF], F32R)
    al = sb("fal", [P, KD, HALF], F32R)
    sa = [sb(f"sa{j}", [P, HALF]) for j in range(2)]
    hf = [sb(f"fhf{j}", [P, HALF]) for j in range(3)]
    hid = [[sb(f"hid{s}{j}", [P, KF, HALF], F32R) for j in range(2)] for s in range(2)]

    with ExitStack() as own:
        bank = [own.enter_context(nc.psum_tensor(f"fbank{j}", [P, 512], F32)) for j in range(FFN_BANKS)]
        front = [own.enter_context(nc.psum_tensor(f"front{j}", [P, 512], F32)) for j in range(KD)]
        block = own.enter_context(nc.Block())

        @block.sync
        def _(sp):
            def load(b, u, row):
                sp.wait_ge(xin.free(u), xin.used_before(b, u))
                sp.sem_inc(s_passed, 1)
                sp.dma_start(fx[u][:], x1_d[row, u * HALF:(u + 1) * HALF, :].rearrange(
                    "(c p) d -> p c d", p=P)).then_inc(xin.full(u), 16)
                if u == 0:
                    with nc.allow_non_contiguous_dma(reason="two small vectors"):
                        sp.dma_start(csh[:], rows(mod_d[row, 3 * D:4 * D], P)).then_inc(c_mod.sem, 16)
                        sp.dma_start(csc[:], rows(mod_d[row, 4 * D:5 * D], P)).then_inc(c_mod.sem, 16)

            load(0, 0, 0)
            with sp.Fori(0, B) as b:
                next_row = sp.snap((b + 1) % B)
                for u in us:
                    nb, nu = after_block(b, u)
                    if u == 0:
                        sp.wait_ge(c_out.sem, c_out.at(b, 0))
                        sp.sem_inc(s_passed, 1)
                        sp.dma_start(gb[:], mod_d[b, 5 * D:6 * D].partition_broadcast(P)).then_inc(c_gbin.sem, 16)
                    if nu == 0:
                        for k in range(KD):
                            sp.wait_ge(fronts.free((u, k)), fronts.used(b, (u, k)))
                    load(nb, nu, b if nu else next_row)
                    sp.wait_ge(c_out.sem, c_out.at(b, u + 1))
                    sp.sem_inc(s_passed, 1)
                    sp.dma_start(g["out"][b, u * HALF:(u + 1) * HALF, :].rearrange("(c p) d -> p c d", p=P),
                                 fx[u][:]).then_inc(xin.free(u), 16)
            for u in us:
                sp.wait_ge(xin.free(u), 16 * B + START)

        @block.tensor
        def _(pe):
            def rows_of_batch(dt):
                def layer(b, u, name, w, halves, wait):
                    for m in range(KF):
                        key = (u, name, m)
                        pe.wait_ge(banks.free(key), banks.used_before(b, key))
                        for k in range(w.shape[1]):
                            if m == 0 and wait is not None:
                                pe.wait_ge(c_lo.sem, c_lo.at(b, wait + k + 1))
                            for n, h in enumerate(halves):
                                mm = pe.matmul(bank[banks.slot(key)][:], w[:, k, m * P:(m + 1) * P].bitcast(dt),
                                               h[:, k, :].bitcast(dt), start=(k + n == 0),
                                               stop=(k == w.shape[1] - 1 and n == 1))
                        mm.then_inc(banks.full(key), 1)

                def transposes(b, u):
                    pe.wait_ge(c_norm.sem, c_norm.at(b, u + 1))
                    for k in range(KD):
                        pe.wait_ge(fronts.free((u, k)), fronts.used_before(b, (u, k)))
                        for c in range(NC):
                            mm = pe.transpose(front[k][:, c * P:(c + 1) * P], nrm[:, c, k * P:(k + 1) * P], ident[:])
                        mm.then_inc(fronts.full((u, k)), 1)

                transposes(0, 0)
                with pe.Fori(0, B) as b:
                    for u in us:
                        pe.wait_ge(c_al.sem, c_al.at(b, u + 1))
                        for m in range(KF):
                            for name, w in (("a", ws[0]), ("g", ws[1])):
                                key = (u, name, m)
                                pe.wait_ge(banks.free(key), banks.used_before(b, key))
                                for k in range(KD):
                                    for n, h in enumerate((ah, al)):
                                        mm = pe.matmul(bank[banks.slot(key)][:],
                                                       w[:, k, m * P:(m + 1) * P].bitcast(dt), h[:, k, :].bitcast(dt),
                                                       start=(k + n == 0), stop=(k == KD - 1 and n == 1))
                                mm.then_inc(banks.full(key), 1)
                        at = 3 * KF * u
                        layer(b, u, "h1", ws[2], hid[0], at)
                        transposes(*after_block(b, u))
                        layer(b, u, "h2", ws[3], hid[1], at + KF)
                        for j in range(NC // 2):
                            key = (u, "o", j)
                            pe.wait_ge(banks.free(key), banks.used_before(b, key))
                            for c in range(2 * j, 2 * j + 2):
                                for k in range(KF):
                                    if c == 0:
                                        pe.wait_ge(c_lo.sem, c_lo.at(b, at + 2 * KF + k + 1))
                                    for n, h in enumerate(hid[0]):
                                        mm = pe.matmul(bank[banks.slot(key)][:, (c % 2) * D:(c % 2 + 1) * D],
                                                       h[:, k, c * P:(c + 1) * P].bitcast(dt),
                                                       ws[4][:, k, :].bitcast(dt), start=(k + n == 0),
                                                       stop=(k == KF - 1 and n == 1))
                            mm.then_inc(banks.full(key), 1)

            differing = pe.value_load(inexact[0:1, 0:1])
            with pe.If(differing == 0):
                rows_of_batch(F32R)
            with pe.Else():
                rows_of_batch(F32)

        @block.scalar
        def _(act):
            def affine(b, u):
                if u == 0:
                    act.wait_ge(c_mod.sem, c_mod.at(b, 32))
                for k in range(KD):
                    act.wait_ge(fronts.full((u, k)), fronts.filled(b, (u, k)))
                    nc.scalar.activation(af[:, k, :], front[k][:], ACT.Identity,
                                         bias=csh[:, k:k + 1], scale=csc[:, k:k + 1]).then_inc(fronts.free((u, k)), 1)

            affine(0, 0)
            with act.Fori(0, B) as b:
                for u in us:
                    for m in range(KF):
                        key = (u, "a", m)
                        act.wait_ge(banks.full(key), banks.filled(b, key))
                        if m >= 2:
                            before = (u, "g", m - 2)
                            act.wait_ge(banks.free(before), banks.used(b, before))
                        nc.scalar.activation(sa[m % 2][:], bank[banks.slot(key)][:], ACT.Silu, scale=s1[:, m:m + 1])\
                            .then_inc(banks.free(key), 1)
                    for i, (name, s) in enumerate((("h1", sh1), ("h2", sh2)), 1):
                        if i == 2:
                            affine(*after_block(b, u))
                        for m in range(KF):
                            key, j = (u, name, m), KF * i + m
                            act.wait_ge(banks.full(key), banks.filled(b, key))
                            act.wait_ge(c_lo.sem, c_lo.at(b, 3 * KF * u + j - 2))
                            nc.scalar.activation(hf[j % 3][:], bank[banks.slot(key)][:], ACT.Gelu,
                                                 scale=s[:, m:m + 1]).then_inc(banks.free(key), 1)

        @block.gpsimd
        def _(pool):
            def power(b, u):
                pool.wait_ge(c_stat.sem, c_stat.at(b, u + 1))
                pool.tensor_tensor(rstd[:], var[:], neg_half[:, 0:NC], ALU.pow).then_inc(c_rstd.sem, 1)

            def high(b, u):
                for k in range(KD):
                    pool.wait_ge(fronts.free((u, k)), fronts.used(b, (u, k)))
                pool.sem_inc(s_fill, 1)
                pool.tensor_scalar(ah[:], af[:], 1.0, 0.0, ALU.mult, ALU.add).then_inc(c_ah.sem, 1)

            power(0, 0)
            high(0, 0)
            with pool.Fori(0, B) as b:
                for u in us:
                    for i, name in enumerate(layers):
                        if i == 2:
                            high(*after_block(b, u))
                        for m in range(KF):
                            if (i, m) == (1, 3):
                                power(*after_block(b, u))
                            j = KF * i + m
                            pool.wait_ge(banks.free((u, name, m)), banks.used(b, (u, name, m)))
                            pool.sem_inc(s_fill, 1)
                            pool.tensor_scalar(hid[i % 2][0][:, m, :], hf[j % 3][:], 1.0, 0.0, ALU.mult, ALU.add)\
                                .then_inc(c_hi.sem, 1)

        @block.vector
        def _(dve):
            def variances(b, u):
                dve.wait_ge(xin.full(u), xin.filled(b, u))
                for c in range(NC):
                    last = dve.bn_stats(stats[:, c, :], fx[u][:, c, :])
                last.then_inc(c_bn.sem, 1)
                dve.wait_ge(c_bn.sem, c_bn.at(b, 2 * u + 1))
                dve.sem_inc(s_const, 1)
                for c in range(NC):
                    last = dve.bn_aggr(mv[:, c, :], stats[:, c, :])
                last.then_inc(c_bn.sem, 1)
                dve.wait_ge(c_bn.sem, c_bn.at(b, 2 * u + 2))
                dve.tensor_scalar(var[:], mv[:, :, 1], EPS, None, ALU.add).then_inc(c_stat.sem, 1)

            def normalise(b, u):
                dve.wait_ge(c_rstd.sem, c_rstd.at(b, u + 1))
                for c in range(NC):
                    last = dve.tensor_scalar(nrm[:, c, :], fx[u][:, c, :], mv[:, c, 0:1], rstd[:, c:c + 1],
                                             ALU.subtract, ALU.mult)
                last.then_inc(c_norm.sem, 1)

            def front_low(b, u):
                for k in range(KD):
                    dve.wait_ge(fronts.free((u, k)), fronts.used(b, (u, k)))
                dve.wait_ge(c_ah.sem, c_ah.at(b, u + 1))
                dve.tensor_tensor(al[:], af[:], ah[:].bitcast(F32), ALU.subtract).then_inc(c_al.sem, 1)

            variances(0, 0)
            normalise(0, 0)
            front_low(0, 0)
            with dve.Fori(0, B) as b:
                for u in us:
                    if u == 0:
                        dve.wait_ge(c_gbin.sem, c_gbin.at(b, 16))
                        dve.tensor_tensor(gb[:], gb[:], s3r[:], ALU.mult).then_inc(c_gb.sem, 1)

                    def low(i, m):
                        j = KF * i + m
                        dve.wait_ge(c_hi.sem, c_hi.at(b, 3 * KF * u + j + 1))
                        dve.tensor_tensor(hid[i % 2][1][:, m, :], hf[j % 3][:], hid[i % 2][0][:, m, :].bitcast(F32),
                                          ALU.subtract).then_inc(c_lo.sem, 1)

                    for m in range(KF):
                        gate_key, key = (u, "a", m), (u, "g", m)
                        dve.wait_ge(banks.free(gate_key), banks.used(b, gate_key))
                        dve.wait_ge(c_lo.sem, c_lo.at(b, max(3 * KF * u + m - 2, 0)))
                        dve.wait_ge(banks.full(key), banks.filled(b, key))
                        dve.scalar_tensor_tensor(out=hf[m % 3][:], in0=bank[banks.slot(key)][:], scalar=s2[:, m:m + 1],
                                                 in1=sa[m % 2][:], op0=ALU.mult, op1=ALU.mult)\
                            .then_inc(banks.free(key), 1)
                        if m:
                            low(0, m - 1)
                    low(0, KF - 1)
                    for i in (1, 2):
                        if i == 2:
                            front_low(*after_block(b, u))
                        for m in range(KF):
                            low(i, m)
                            if (i, m) == (1, 1):
                                variances(*after_block(b, u))
                            if (i, m) == (1, 4):
                                normalise(*after_block(b, u))
                    if u == 0:
                        dve.wait_ge(c_gb.sem, c_gb.at(b, 1))
                    for j in range(NC // 2):
                        key, cc = (u, "o", j), slice(2 * j, 2 * j + 2)
                        dve.wait_ge(banks.full(key), banks.filled(b, key))
                        dve.tensor_tensor(go[:, cc, :], bank[banks.slot(key)][:].rearrange("p (c d) -> p c d", c=2),
                                          gb[:].unsqueeze(1).to_broadcast([P, 2, D]), ALU.mult)\
                            .then_inc(banks.free(key), 1)
                    dve.wait_ge(banks.free(key), banks.used(b, key))
                    dve.wait_ge(banks.free((u, "o", 0)), banks.used(b, (u, "o", 0)))
                    dve.tensor_tensor(fx[u][:], fx[u][:], go[:], ALU.add).then_inc(c_out.sem, 1)


def kernel(**inputs):
    import numpy as np
    import concourse.bacc as bacc
    from concourse.bass_utils import run_bass_kernel_spmd as run

    nc = bacc.Bacc("TRN2", target_bir_lowering=False, num_devices=1)
    a = {k[3:]: np.asarray(v) for k, v in inputs.items()}
    t = np.ascontiguousarray
    arrays = dict(
        x=a["attn_x"], ln_w=a["attn_ln_w"], ln_b=a["attn_ln_b"], w_in=a["attn_in_proj_w"], conv_w=a["attn_conv_w"],
        conv_b=a["attn_conv_b"], dt_bias=a["attn_dt_bias"], a_log=a["attn_A_log"], d_skip=a["attn_D_skip"],
        rms_w=a["attn_rms_w"], w_out=a["attn_out_proj_w"], m1=a["attn_mlp_w1"], b1=a["attn_mlp_b1"],
        m2=a["attn_mlp_w2"], b2=a["attn_mlp_b2"], w1=t(a["ffn_w1_w"].T), s1=a["ffn_w1_s"], w2=t(a["ffn_w2_w"].T),
        s2=a["ffn_w2_s"], h1=t(a["ffn_h1_w"].T), sh1=a["ffn_h1_s"], h2=t(a["ffn_h2_w"].T), sh2=a["ffn_h2_s"],
        w3=t(a["ffn_w3_w"].T), s3=a["ffn_w3_s"], cT=t(a["c"].T), wmod=a["wmod"])
    arrays = {f"in_{k}": t(v) for k, v in arrays.items()}
    args = {k[3:]: nc.dram_tensor(k, v.shape, mybir.dt.from_np(v.dtype), kind="ExternalInput").ap()
            for k, v in arrays.items()}
    out = nc.dram_tensor("out_x", (B, L, D), F32, kind="ExternalOutput").ap()
    build(nc, **args, out=out)
    return run(nc, [arrays], core_ids=[0]).results[0]["out_x"]
```

```python
from contextlib import ExitStack

import concourse.bass as bass
from concourse import mybir

ALU = mybir.AluOpType
ACT = mybir.ActivationFunctionType
AX = mybir.AxisListType
F32 = mybir.dt.float32
F32R = mybir.dt.float32r
BF16 = mybir.dt.bfloat16
I32 = mybir.dt.int32

P = 128
B, L, D = 8, 1024, 256
HALF = 512
NU = L // HALF
NC = HALF // P
KD = D // P
NH, HD, DS = 32, 16, 128
DI = NH * HD
QI = DI // P
HQ = P // HD
XM = (DI + 2 * DS) // P
CONV = DI + 2 * DS
TAPS = 4
ZX = 2 * DI + 2 * DS
FF = 1024
KF = FF // P
G4 = 4
NG = NH // G4
EPS = 1e-5
PROJ = (*range(QI, 2 * QI + 2), *range(QI))
SERIES = 7


START = 1


def start(eng, counts):
    for count in counts:
        for s in count.sems:
            eng.sem_inc(s, START)


class Handover:

    def __init__(self, sem, name, keys, slots, fills=1, uses=1, both=True):
        self.full_sems = [sem(f"{name}_full{i}") for i in range(slots)]
        self.free_sems = [sem(f"{name}_free{i}") for i in range(slots)] if both else None
        self.place = {k: (i % slots, i // slots) for i, k in enumerate(keys)}
        self.rounds = [len(range(i, len(keys), slots)) for i in range(slots)]
        self.fills, self.uses = fills, uses
        self.sems = self.full_sems + (self.free_sems or [])

    def slot(self, key):
        return self.place[key][0]

    def full(self, key):
        return self.full_sems[self.slot(key)]

    def free(self, key):
        return self.free_sems[self.slot(key)]

    def turn(self, b, key):
        s, n = self.place[key]
        return b * self.rounds[s] + n

    def filled(self, b, key):
        return (self.turn(b, key) + 1) * self.fills + START

    def filled_before(self, b, key):
        return self.turn(b, key) * self.fills + START

    def used(self, b, key):
        return (self.turn(b, key) + 1) * self.uses + START

    def used_before(self, b, key):
        return self.turn(b, key) * self.uses + START


class Count:

    def __init__(self, sem, name, per):
        self.sem, self.per = sem(name), per
        self.sems = [self.sem]

    def at(self, b, n):
        return b * self.per + n + START


class Steps(Count):

    def __init__(self, sem, name, per):
        super().__init__(sem, name, per)
        self.n = 0

    def mark(self, ins):
        ins.then_inc(self.sem, 1)
        self.n += 1
        return self.n

    def closed(self):
        assert self.n == self.per, (self.n, self.per)


def mamba_bank_order():
    for u in range(NU):
        yield from ((u, "in", m) for m in PROJ)
        yield (u, "dtw")
        yield (u, "dec")
        yield from ((u, "ec", q) for q in range(QI))
        yield (u, "xT", 0)
        yield (u, "bt", 0)
        for c in range(NC):
            if c >= 2:
                yield (u, "op", c - 2)
            yield (u, "st", c)
            if c + 1 < NC:
                yield (u, "xT", c + 1)
                yield (u, "bt", c + 1)
        yield (u, "op", NC - 2)
        yield (u, "op", NC - 1)
        yield from ((u, "mT", k) for k in range(KD))
        yield from ((u, "m1", m) for m in range(KF))
        yield from ((u, "m2", j) for j in range(NC // 2))


def ffn_bank_order():
    for u in range(NU):
        for m in range(KF):
            yield (u, "a", m)
            yield (u, "g", m)
        yield from ((u, "h1", m) for m in range(KF))
        yield from ((u, "h2", m) for m in range(KF))
        yield from ((u, "o", j) for j in range(NC // 2))


DVE_STEPS = 35
FRONT_STEPS = 26
POOL_CONV = 1
HF = 4
RING = 4
LAG = 3


def after_block(b, u):
    return (b, u + 1) if u < NU - 1 else (b + 1, 0)


def build(nc, x, ln_w, ln_b, w_in, conv_w, conv_b, dt_bias, a_log, d_skip, rms_w, w_out, m1, b1, m2,
          b2, w1, s1, w2, s2, h1, sh1, h2, sh2, w3, s3, cT, wmod, out):
    top = ExitStack()
    with top:
        def sem(name):
            return top.enter_context(nc.semaphore(name))

        def keep(name, shape, dt=F32):
            return top.enter_context(nc.sbuf_tensor(name, shape, dt))

        mod_d = nc.dram_tensor("mod_d", [B, 6 * D], F32, kind="Internal").ap()
        x1_d = nc.dram_tensor("x1_d", [B, L, D], F32, kind="Internal").ap()
        ffn_d = [nc.dram_tensor(n, [P, k * n_], F32, kind="Internal").ap()
                 for n, k, n_ in (("w1_d", KD, FF), ("w2_d", KD, FF), ("h1_d", KF, FF),
                                  ("h2_d", KF, FF), ("w3_d", KF, D))]

        s_fill, s_const = sem("pool_constants"), sem("dve_constants")
        ident = keep("ident", [P, P])
        ones = keep("ones", [P, P])
        neg_half = keep("neg_half", [P, 4])

        g = dict(s_fill=s_fill, s_const=s_const, ident=ident, ones=ones, neg_half=neg_half, mod_d=mod_d, x1_d=x1_d, ffn_d=ffn_d, x=x,
                 ln_w=ln_w, ln_b=ln_b, w_in=w_in, conv_w=conv_w, conv_b=conv_b, dt_bias=dt_bias,
                 a_log=a_log, d_skip=d_skip, rms_w=rms_w, w_out=w_out, m1=m1, b1=b1, m2=m2, b2=b2,
                 w1=w1, s1=s1, w2=w2, s2=s2, h1=h1, sh1=sh1, h2=h2, sh2=sh2, w3=w3, s3=s3, cT=cT,
                 wmod=wmod, out=out)
        with ExitStack() as ctx:
            mamba(nc, ctx, sem, g)
        with ExitStack() as ctx:
            feed_forward(nc, ctx, sem, g)


def rows(v, n):
    return v.rearrange("(m p) -> p m", p=n)


def mamba(nc, ctx, sem, g):
    ident, ones, neg_half = g["ident"], g["ones"], g["neg_half"]
    mod_d, x1_d = g["mod_d"], g["x1_d"]
    s_fill, s_const = g["s_fill"], g["s_const"]

    def sb(name, shape, dt=F32):
        return ctx.enter_context(nc.sbuf_tensor(name, shape, dt))

    win = [sb(f"win{j}", [P, KD, ZX], F32R) for j in range(2)]
    wout = [sb(f"wout{j}", [P, QI, D], F32R) for j in range(2)]
    wm1 = [sb(f"wm1{j}", [P, KD, FF], F32R) for j in range(2)]
    wm2 = [sb(f"wm2{j}", [P, KF, D], F32R) for j in range(2)]
    wdt = sb("wdt", [P, KD, NH])
    lnw = sb("lnw", [P, KD])
    lnb = sb("lnb", [P, KD])
    cw = sb("cw", [P, XM, TAPS])
    cb = sb("cb", [P, XM])
    rmsw = sb("rmsw", [P, QI])
    b1c = sb("b1c", [P, KF])
    b2r = sb("b2r", [P, D])
    dtb = sb("dtb", [P, 1])
    nega = sb("nega", [P, 1])
    dsk = sb("dsk", [P, QI])
    tri = sb("tri", [P, P])
    pick = sb("pick", [96, QI, P], BF16)
    cleft = sb("cleft", [99, NC, P], BF16)
    cright = [sb(f"cright{j}", [99, NH, P], BF16) for j in range(2)]
    state = sb("state", [P, DI])
    cin = sb("cin", [P, XM, TAPS - 1 + HALF])
    xpad = [sb(f"xpad{j}", [P, NH // 2, 2, 2, HD]) for j in range(2)]

    us, ucs = range(NU), [(u, c) for u in range(NU) for c in range(NC)]
    groups = [(u, c, i) for u, c in ucs for i in range(NG)]
    banks = Handover(sem, "bank", list(mamba_bank_order()), 4)
    xin = Handover(sem, "x", list(us), 2, fills=16, uses=16)
    h_shsc = Handover(sem, "shsc", [0], 1, fills=16, both=False)
    h_gate = Handover(sem, "gate", [0], 1, fills=16, both=False)
    h_es = Handover(sem, "decay", groups, RING, both=False)
    h_mh = Handover(sem, "mh", groups, RING)
    h_right = Handover(sem, "cright", ucs, 2, fills=48, both=False)
    h_yoff = Handover(sem, "yoff", [k for k in ucs if k != (0, 0)], 1)
    c_yused = Count(sem, "yaddends_used", NU * NC)
    h_yhl = Handover(sem, "yhalves", ucs, 1, both=False)
    h_eb = Handover(sem, "ebank", [k for u in us for k in (*((u, "nT", j) for j in range(KD)), (u, "dt"),
                                                          *(g_ for g_ in groups if g_[0] == u))], 2)
    c_yread = Count(sem, "yin_read", NU * NC)
    c_stat = Count(sem, "variance_made", NU * (3 + NC))
    c_rstd = Count(sem, "rstd_made", NU * (3 + NC))
    c_norm = Count(sem, "norm_made", NU * 2)
    c_ah = Count(sem, "act_hi_made", NU * 2 * KD)
    c_al = Count(sem, "act_lo_made", NU * 2 * KD)
    c_cacc = Count(sem, "conv_made", NU * (XM - POOL_CONV))
    c_pacc = Count(sem, "pool_conv_made", NU * POOL_CONV)
    c_ptap = Count(sem, "pool_taps", NU * POOL_CONV * (2 * TAPS - 3))
    c_xc = Count(sem, "xc_made", NU * XM)
    c_dexp = Count(sem, "dexp_made", NU)
    c_cum = Count(sem, "cum_parts_made", NU)
    c_wexp = Count(sem, "wexp_made", NU)
    c_wv = Count(sem, "wv_made", NU)
    c_left = Count(sem, "cleft_made", NU)
    c_yg = Count(sem, "y_gated", NU * NC)
    c_yh = Count(sem, "y_hi_made", NU * NC)
    c_ysum = Count(sem, "y_squares_summed", NU * NC)
    c_ysq = Count(sem, "y_squared", NU * NC)
    c_hh = Count(sem, "hidden_hi_made", NU * KF)
    c_hl = Count(sem, "hidden_lo_made", NU * KF)
    c_o1 = Count(sem, "o1_biased", NU)
    c_x1 = Count(sem, "x1_made", NU)
    s_passed = sem("passed")
    s_copy = sem("ffn_weights_copied")
    own_dve = Steps(sem, "dve_steps", DVE_STEPS)
    own_front = Count(sem, "front_steps", NU * FRONT_STEPS)
    c_dabs = Count(sem, "dabs_made", NU)
    counts = [v for v in locals().values() if isinstance(v, (Handover, Count))]

    with ExitStack() as own:
        def tmp(name, shape, dt=F32):
            return own.enter_context(nc.sbuf_tensor(name, shape, dt))

        stage = tmp("stage", [P, KD * ZX])
        ct = tmp("ct", [P, KD, B])
        wm = tmp("wm", [P, KD, 6 * D])
        mod = tmp("mod", [B, 6 * D])
        ga_a = tmp("ga_a", [B, 2, D])
        mp = own.enter_context(nc.psum_tensor("mp", [B, 3, 512], F32))
        s_vec = sem("s_vec")
        s_small = sem("s_small")
        s_stage = sem("s_stage")
        s_split = sem("s_split")
        s_ct = sem("s_ct")
        s_silu = sem("s_silu")
        s_mod = sem("s_mod")
        s_modrow = sem("s_modrow")
        s_store = sem("s_store")
        s_a = sem("s_a")
        splits = [(g["w_in"][:, 0:ZX].rearrange("(k p) n -> p k n", p=P), win, KD, ZX),
                  (g["w_out"].rearrange("(k p) n -> p k n", p=P), wout, QI, D),
                  (g["m1"].rearrange("(k p) n -> p k n", p=P), wm1, KD, FF),
                  (g["m2"].rearrange("(k p) n -> p k n", p=P), wm2, KF, D)]
        block = own.enter_context(nc.Block())

        @block.sync
        def _(sp):
            start(sp, counts)
            sp.dma_start(ct[:], g["cT"].rearrange("(k p) b -> p k b", p=P)).then_inc(s_ct, 16)
            sp.dma_start(wm[:], g["wmod"].rearrange("(k p) n -> p k n", p=P)).then_inc(s_ct, 16)
            for i, (src, _, k, n) in enumerate(splits):
                if i:
                    sp.wait_ge(s_split, 2 * i)
                sp.dma_start(stage[:, 0:k * n].rearrange("p (k n) -> p k n", k=k), src).then_inc(s_stage, 16)
            sp.wait_ge(s_modrow, 6)
            sp.dma_start(mod_d, mod[:]).then_inc(s_store, 16)
            sp.wait_ge(s_store, 16)

        @block.scalar
        def _(act):
            vecs = [(lnw[:], rows(g["ln_w"], P)), (lnb[:], rows(g["ln_b"], P)),
                    (cw[:], g["conv_w"].rearrange("(m p) k -> p m k", p=P)), (cb[:], rows(g["conv_b"], P)),
                    (rmsw[:], rows(g["rms_w"], P)), (b1c[:], rows(g["b1"], P)),
                    (b2r[:], g["b2"].partition_broadcast(P)),
                    (wdt[:], g["w_in"][:, ZX:ZX + NH].rearrange("(k p) n -> p k n", p=P))]
            for c in range(NC):
                vecs.append((dtb[NH * c:NH * c + NH, :], rows(g["dt_bias"], NH)))
                vecs.append((nega[NH * c:NH * c + NH, :], rows(g["a_log"], NH)))
            for h in range(HQ):
                vecs.append((dsk[HD * h:HD * h + HD, :],
                             g["d_skip"].rearrange("(q h) -> h q", h=HQ)[h].partition_broadcast(HD)))
            with nc.allow_non_contiguous_dma(reason="a few small vectors"):
                for dst, src in vecs:
                    act.dma_start(dst, src).then_inc(s_vec, 16)
            act.wait_ge(s_ct, 32)
            nc.scalar.activation(ct[:], ct[:], ACT.Silu).then_inc(s_silu, 1)
            act.wait_ge(s_vec, 16 * len(vecs))
            nc.scalar.activation(nega[:], nega[:], ACT.Exp).then_inc(s_a, 1)

        @block.tensor
        def _(pe):
            pe.wait_ge(s_silu, 1)
            for j in range(3):
                for k in range(KD):
                    mm = pe.matmul(mp[:, j, :], ct[:, k, :], wm[:, k, j * 512:(j + 1) * 512],
                                   start=(k == 0), stop=(k == KD - 1))
            mm.then_inc(s_mod, 1)

        @block.vector
        def _(dve):
            dve.memset(ones[:], 1.0).then_inc(s_const, 1)
            dve.memset(neg_half[:], -0.5)
            dve.memset(cin[:], 0.0)
            for j in range(2):
                dve.memset(xpad[j][:], 0.0)
            dve.wait_ge(s_mod, 1)
            mod_p = mp[:, :, :].rearrange("b j n -> b (j n)")
            for j in (0, 3):
                dve.tensor_copy(mod[:, j * D:(j + 1) * D], mod_p[:, j * D:(j + 1) * D]).then_inc(s_modrow, 1)
            for j in (1, 4):
                dve.tensor_scalar(mod[:, j * D:(j + 1) * D], mod_p[:, j * D:(j + 1) * D], 1.0, None,
                                  ALU.add).then_inc(s_modrow, 1)
            for i, j in enumerate((2, 5)):
                gp = mod_p[:, j * D:(j + 1) * D]
                dve.tensor_scalar(ga_a[:, 0, :], gp, 0.0, 2.0, ALU.is_ge, ALU.mult).then_inc(s_small, 1)
                dve.tensor_scalar(ga_a[:, 1, :], gp, -1.0, None, ALU.mult).then_inc(s_small, 1)
                dve.wait_ge(s_small, 5 * i + 2)
                dve.tensor_scalar(ga_a[:, 0, :], ga_a[:, 0, :], 1.0, None, ALU.subtract).then_inc(s_small, 1)
                dve.tensor_tensor(ga_a[:, 1, :], gp, ga_a[:, 1, :], ALU.max).then_inc(s_small, 1)
                dve.wait_ge(s_small, 5 * i + 4)
                dve.tensor_scalar(ga_a[:, 1, :], ga_a[:, 1, :], 0.25, None, ALU.max).then_inc(s_small, 1)
                dve.wait_ge(s_small, 5 * i + 5)
                dve.tensor_tensor(mod[:, j * D:(j + 1) * D], ga_a[:, 0, :], ga_a[:, 1, :],
                                  ALU.mult).then_inc(s_modrow, 1)
                dve.wait_ge(s_modrow, 5 + i)
            dve.wait_ge(s_a, 1)
            dve.tensor_scalar(nega[:], nega[:], -1.0, None, ALU.mult)
            for i, (_, halves, k, n) in enumerate(splits):
                dve.wait_ge(s_stage, 16 * (i + 1))
                w = stage[:, 0:k * n].rearrange("p (k n) -> p k n", k=k)
                if i == 1:
                    dve.wait_ge(s_vec, 16)
                    for q in range(k):
                        last = dve.tensor_scalar(w[:, q, :], w[:, q, :], rmsw[:, q:q + 1], None, ALU.mult)
                    last.then_inc(s_const, 1)
                    dve.wait_ge(s_const, 2)
                dve.tensor_copy(halves[0][:], w).then_inc(s_split, 1)
                dve.wait_ge(s_split, 2 * i + 1)
                dve.tensor_tensor(halves[1][:], w, halves[0][:].bitcast(F32), ALU.subtract).then_inc(s_split, 1)

        @block.gpsimd
        def _(pool):
            pool.memset(ident[:], 0.0)
            pool.memset(tri[:], 1.0)
            pool.memset(pick[:], 0.0)
            pool.memset(cleft[:], 0.0)
            for j in range(2):
                last = pool.memset(cright[j][:], 0.0)
            last.then_inc(s_fill, 1)
            pool.wait_ge(s_fill, 1)
            pool.memset(cleft[96:99, :, :], 1.0).then_inc(s_fill, 1)
            pool.wait_ge(s_fill, 2)
            pool.affine_select(out=ident[:], in_=ident[:], compare_op=ALU.not_equal, fill=1.0, base=0,
                               pattern=[[-1, P]], channel_multiplier=1)
            pool.affine_select(out=tri[:], in_=tri[:], compare_op=ALU.is_ge, fill=0.0, base=0,
                               pattern=[[1, P]], channel_multiplier=-1).then_inc(s_fill, 1)
            pool.wait_ge(s_fill, 3)
            for j in range(3):
                v = pick[:].rearrange("k q (h d) -> k (q h) d", d=HD)
                pool.affine_select(out=v, in_=v, compare_op=ALU.not_equal, fill=1.0, base=-NH * j,
                                   pattern=[[-1, NH], [0, HD]], channel_multiplier=1)
                for r in range(2):
                    v = cright[r][0:96, :, :]
                    last = pool.affine_select(out=v, in_=v, compare_op=ALU.not_equal, fill=-1.0,
                                              base=-NH * j, pattern=[[-1, NH], [0, P]], channel_multiplier=1)
                last.then_inc(s_fill, 1)
                pool.wait_ge(s_fill, 4 + j)

    xs = [sb(f"xs{u}", [P, NC, D]) for u in range(NU)]
    shsc = sb("shsc", [P, 2, D])
    gate = sb("gate", [P, D])
    res = sb("res", [P, NC, D])
    nrm = sb("nrm", [P, NC, D])
    stats = sb("stats", [P, NC, 6])
    mv = sb("mv", [P, NC, 2])
    var = sb("var", [P, NC])
    rstd = sb("rstd", [P, NC])
    af = sb("af", [P, KD, HALF])
    ah = sb("ah", [P, KD, HALF], F32R)
    al = sb("al", [P, KD, HALF], F32R)
    dabs = sb("dabs", [P, P])
    dexp = dabs
    drelu = sb("drelu", [P, P])
    dden = sb("dden", [P, P])
    ds_ = sb("ds_", [P, P])
    dsq = sb("dsq", [P, P])
    dser = sb("dser", [P, P])
    dtv = sb("dtv", [P, P])
    da = dden
    cum = sb("cum", [P, P])
    crest = sb("crest", [P, 2, P])
    parts = sb("parts", [P, 3, P], BF16)
    wexp = sb("wexp", [P, P])
    wv = sb("wv", [P, P])
    cend = sb("cend", [P, 1])
    dend = sb("dend", [P, P])
    dtw = sb("dtw", [P, 2, NC, NH])
    dec = sb("dec", [P, NC, NH])
    xw = [sb(f"xw{j}", [P, DI]) for j in range(2)]
    bt = [sb(f"bt{j}", [P, P]) for j in range(2)]
    gm = [sb(f"gm{j}", [P, P]) for j in range(2)]
    mh = [sb(f"mh{j}", [P, G4, P]) for j in range(RING)]
    yoff_s = sb("yoff_s", [P, QI, P])
    yin_s = sb("yin_s", [P, QI, P])
    yg = sb("yg", [P, QI, P])
    ysq = yoff_s
    ysum = sb("ysum", [P, P])
    yh = sb("yh", [P, QI, P], F32R)
    yl = sb("yl", [P, QI, P], F32R)
    ms = sb("ms", [P, 1])
    rms = sb("rms", [P, 1])
    hf = [sb(f"hf{j}", [P, HALF]) for j in range(2)]
    o1 = sb("o1", [P, NC, D])

    with ExitStack() as mixer:
        def mx(name, shape, dt=F32):
            return mixer.enter_context(nc.sbuf_tensor(name, shape, dt))

        sz = mx("sz", [P, QI, HALF])
        ec = mx("ec", [P, QI, HALF])
        xc = mx("xc", [P, XM, HALF])
        cacc = [mx(f"cacc{j}", [P, HALF]) for j in range(2)]
    es = [t[:].rearrange("s (h t) -> s h t", h=G4) for t in (*cacc, *hf)]
    cacc = [*cacc, *(t[:].rearrange("s h t -> s (h t)") for t in mh)]
    hf = [*hf, *(mh[j][:].rearrange("s h t -> s (h t)") for j in range(HF - 2))]
    hh = sb("hh", [P, KF, HALF], F32R)
    hl = sb("hl", [P, KF, HALF], F32R)

    with ExitStack() as own:
        bank = [own.enter_context(nc.psum_tensor(f"bank{j}", [P, 512], F32)) for j in range(4)]
        eb = [own.enter_context(nc.psum_tensor(f"eb{j}", [P, 512], F32)) for j in range(2)]
        yin = own.enter_context(nc.psum_tensor("yin", [P, QI, P], F32))
        yoff = own.enter_context(nc.psum_tensor("yoff", [P, QI, P], F32))

        block = own.enter_context(nc.Block())

        @block.sync
        def _(sp):
            def load(b, u, row):
                sp.wait_ge(xin.free(u), xin.used_before(b, u))
                sp.sem_inc(s_passed, 1)
                sp.dma_start(xs[u][:], g["x"][row, u * HALF:(u + 1) * HALF, :].rearrange(
                    "(c p) d -> p c d", p=P)).then_inc(xin.full(u), 16)
                if u == 0:
                    sp.dma_start(shsc[:], mod_d[row, 0:2 * D].rearrange("(j d) -> j d", d=D)
                                 .partition_broadcast(P)).then_inc(h_shsc.full(0), 16)

            load(0, 0, 0)
            with sp.Fori(0, B) as b:
                next_row = sp.snap((b + 1) % B)
                for u in us:
                    nb, nu = after_block(b, u)
                    if u == 0:
                        sp.wait_ge(c_x1.sem, c_x1.at(b, 0))
                        sp.sem_inc(s_passed, 1)
                        sp.dma_start(gate[:], mod_d[b, 2 * D:3 * D].partition_broadcast(P)).then_inc(h_gate.full(0), 16)
                    if nu == 0:
                        sp.wait_ge(c_norm.sem, c_norm.at(b, 2 * u + 1))
                        sp.sem_inc(s_passed, 1)
                    load(nb, nu, b if nu else next_row)
                    if u == 0:
                        for name, dst in zip(("w1", "w2", "h1", "h2", "w3"), g["ffn_d"]):
                            k = dst.shape[1] // g[name].shape[1]
                            sp.dma_start(dst.rearrange("(s p) (k n) -> s p k n", s=B, k=k)[b],
                                         g[name].rearrange("(k s p) n -> s p k n", k=k, s=B)[b]).then_inc(s_copy, 16)
                    sp.wait_ge(c_cum.sem, c_cum.at(b, u + 1))
                    for c in range(NC):
                        key = (u, c)
                        if c >= 2:
                            sp.wait_ge(h_mh.free((u, c - 2, NG - 1)), h_mh.used(b, (u, c - 2, NG - 1)))
                        for j in range(3):
                            sp.dma_start(cright[c % 2][96 + j:97 + j, :, :],
                                         parts[NH * c:NH * c + NH, j, :]).then_inc(h_right.full(key), 16)
                    sp.wait_ge(c_x1.sem, c_x1.at(b, u + 1))
                    sp.sem_inc(s_passed, 1)
                    sp.dma_start(x1_d[b, u * HALF:(u + 1) * HALF, :].rearrange("(c p) d -> p c d", p=P),
                                 xs[u][:]).then_inc(xin.free(u), 16)
            for u in us:
                sp.wait_ge(xin.free(u), 16 * B + START)
            sp.wait_ge(s_copy, 80 * B)

        @block.tensor
        def _(pe):
            def product(o, left, right, first=True, last=True):
                for n, (a, c) in enumerate(((0, 0), (0, 1), (1, 0))):
                    mm = pe.matmul(o, left[a], right[c], start=(first and n == 0), stop=(last and n == 2))
                return mm

            def front(b, u):
                pe.wait_ge(c_norm.sem, c_norm.at(b, 2 * u + 1))
                for k in range(KD):
                    key = (u, "nT", k)
                    pe.wait_ge(h_eb.free(key), h_eb.used_before(b, key))
                    for c in range(NC):
                        mm = pe.transpose(eb[h_eb.slot(key)][:, c * P:(c + 1) * P],
                                          nrm[:, c, k * P:(k + 1) * P], ident[:])
                    mm.then_inc(h_eb.full(key), 1)

            def front_dt(b, u):
                key = (u, "dt")
                for k in range(KD):
                    pe.wait_ge(h_eb.free((u, "nT", k)), h_eb.used(b, (u, "nT", k)))
                pe.wait_ge(h_eb.free(key), h_eb.used_before(b, key))
                for c in range(NC):
                    for k in range(KD):
                        mm = pe.matmul(eb[h_eb.slot(key)][NH * c:NH * c + NH, 0:P], wdt[:, k, :],
                                       af[:, k, c * P:(c + 1) * P], start=(k == 0), stop=(k == KD - 1),
                                       tile_position=(0, NH * c))
                mm.then_inc(h_eb.full(key), 1)

            front(0, 0)
            front_dt(0, 0)
            with pe.Fori(0, B) as b:
                for u in us:
                    for m in PROJ:
                        key = (u, "in", m)
                        pe.wait_ge(banks.free(key), banks.used_before(b, key))
                        for k in range(KD):
                            if m == PROJ[0]:
                                pe.wait_ge(c_al.sem, c_al.at(b, 2 * KD * u + k + 1))
                            mm = product(bank[banks.slot(key)][:], [w[:, k, m * P:(m + 1) * P] for w in win],
                                         [a[:, k, :] for a in (ah, al)], k == 0, k == KD - 1)
                        mm.then_inc(banks.full(key), 1)

                    key = (u, "dtw")
                    pe.wait_ge(c_wv.sem, c_wv.at(b, u + 1))
                    pe.wait_ge(banks.free(key), banks.used_before(b, key))
                    pe.transpose(bank[banks.slot(key)][:, 0:P], dtv[:], ident[:])
                    pe.transpose(bank[banks.slot(key)][:, P:2 * P], wv[:], ident[:]).then_inc(banks.full(key), 1)
                    key = (u, "dec")
                    pe.wait_ge(banks.free(key), banks.used_before(b, key))
                    pe.matmul(bank[banks.slot(key)][:, 0:P], ones[:], dend[:], start=True, stop=True)\
                        .then_inc(banks.full(key), 1)
                    pe.wait_ge(c_left.sem, c_left.at(b, u + 1))
                    for q in range(QI):
                        key = (u, "ec", q)
                        pe.wait_ge(banks.free(key), banks.used_before(b, key))
                        pe.matmul(bank[banks.slot(key)][:], pick[:, q, :],
                                  cleft[0:96, :, :].rearrange("k c t -> k (c t)"), start=True, stop=True)\
                            .then_inc(banks.full(key), 1)

                    def by_token(c):
                        key = (u, "xT", c)
                        pe.wait_ge(banks.free(key), banks.used_before(b, key))
                        for q in range(QI):
                            mm = pe.transpose(bank[banks.slot(key)][:, q * P:(q + 1) * P],
                                              xc[:, q, c * P:(c + 1) * P], ident[:])
                        mm.then_inc(banks.full(key), 1)
                        key = (u, "bt", c)
                        pe.wait_ge(banks.free(key), banks.used_before(b, key))
                        pe.transpose(bank[banks.slot(key)][:, 0:P], xc[:, QI, c * P:(c + 1) * P], ident[:])
                        pe.matmul(bank[banks.slot(key)][:, P:2 * P], xc[:, QI, c * P:(c + 1) * P],
                                  xc[:, QI + 1, c * P:(c + 1) * P], start=True, stop=True)\
                            .then_inc(banks.full(key), 1)

                    def decay(c, i):
                        key = (u, c, i)
                        pe.wait_ge(h_eb.free(key), h_eb.used_before(b, key))
                        mm = pe.matmul(eb[h_eb.slot(key)][:], cleft[:, c, :],
                                       cright[c % 2][:, G4 * i:G4 * (i + 1), :].rearrange("k h t -> k (h t)"),
                                       start=True, stop=True)
                        mm.then_inc(h_eb.full(key), 1)

                    def intra(c, i):
                        key = (u, c, i)
                        pe.wait_ge(h_mh.full(key), h_mh.filled(b, key))
                        for j in range(G4):
                            h = G4 * i + j
                            row = HD * 2 * (h % HQ // 2)
                            mm = pe.matmul(yin[row:row + 2 * HD, h // HQ, :],
                                           xpad[c % 2][:, h // 2, h % 2, :, :].rearrange("s w d -> s (w d)"),
                                           mh[i % RING][:, j, :], start=(h % 2 == 0), stop=(h % 2 == 1),
                                           tile_position=(0, row))
                        mm.then_inc(h_mh.free(key), 1)

                    def from_state(c):
                        last = (u, "st", c - 1) if c else (u - 1, "st", NC - 1)
                        pe.wait_ge(banks.free(last), banks.used(b, last))
                        pe.wait_ge(h_yoff.free((u, c)), h_yoff.used_before(b, (u, c)))
                        for q in range(QI):
                            mm = pe.matmul(yoff[:, q, :], state[:, q * P:(q + 1) * P],
                                           xc[:, QI + 1, c * P:(c + 1) * P], start=True, stop=True)
                        mm.then_inc(h_yoff.full((u, c)), 1)

                    def project(c):
                        key = (u, "op", c)
                        pe.wait_ge(h_yhl.full((u, c)), h_yhl.filled(b, (u, c)))
                        pe.wait_ge(banks.free(key), banks.used_before(b, key))
                        for q in range(QI):
                            product(bank[banks.slot(key)][:, 0:D], [y[:, q, :] for y in (yh, yl)],
                                    [w[:, q, :] for w in wout], q == 0, q == QI - 1)
                        pe.wait_ge(c_ysum.sem, c_ysum.at(b, NC * u + c + 1))
                        pe.matmul(bank[banks.slot(key)][:, D:D + 1], ysum[:], ones[:, 0:1], start=True, stop=True)\
                            .then_inc(banks.full(key), 1)

                    pe.wait_ge(c_xc.sem, c_xc.at(b, XM * (u + 1)))
                    by_token(0)
                    for n in range(NC * NG + LAG):
                        c, i = divmod(n, NG)
                        if c < NC:
                            if i == 0:
                                pe.wait_ge(h_right.full((u, c)), h_right.filled(b, (u, c)))
                            decay(c, i)
                        c, i = divmod(n - LAG, NG)
                        if c >= 0:
                            if i == 0:
                                pe.wait_ge(banks.free((u, "bt", c)), banks.used(b, (u, "bt", c)))
                                pe.wait_ge(c_yread.sem, c_yread.at(b, NC * u + c))
                            intra(c, i)
                            if i == 0 and (u, c) != (0, 0):
                                from_state(c)
                            if i == 1:
                                key = (u, "st", c)
                                pe.wait_ge(banks.free(key), banks.used_before(b, key))
                                pe.matmul(bank[banks.slot(key)][:], bt[c % 2][:], xw[c % 2][:], start=True,
                                          stop=True).then_inc(banks.full(key), 1)
                            if i == 2 and c + 1 < NC:
                                by_token(c + 1)
                            if i == NG - 1 and c:
                                project(c - 1)
                    project(NC - 1)

                    pe.wait_ge(c_norm.sem, c_norm.at(b, 2 * u + 2))
                    for k in range(KD):
                        key = (u, "mT", k)
                        pe.wait_ge(banks.free(key), banks.used_before(b, key))
                        for c in range(NC):
                            mm = pe.transpose(bank[banks.slot(key)][:, c * P:(c + 1) * P],
                                              nrm[:, c, k * P:(k + 1) * P], ident[:])
                        mm.then_inc(banks.full(key), 1)
                    for m in range(KF):
                        key = (u, "m1", m)
                        pe.wait_ge(banks.free(key), banks.used_before(b, key))
                        for k in range(KD):
                            if m == 0:
                                pe.wait_ge(c_al.sem, c_al.at(b, 2 * KD * u + KD + k + 1))
                            mm = product(bank[banks.slot(key)][:], [w[:, k, m * P:(m + 1) * P] for w in wm1],
                                         [a[:, k, :] for a in (ah, al)], k == 0, k == KD - 1)
                        mm.then_inc(banks.full(key), 1)
                    front(*after_block(b, u))
                    for j in range(NC // 2):
                        key = (u, "m2", j)
                        pe.wait_ge(banks.free(key), banks.used_before(b, key))
                        for c in range(2 * j, 2 * j + 2):
                            if c == 1:
                                front_dt(*after_block(b, u))
                            for k in range(KF):
                                if c == 0:
                                    pe.wait_ge(c_hl.sem, c_hl.at(b, KF * u + k + 1))
                                mm = product(bank[banks.slot(key)][:, (c % 2) * D:(c % 2 + 1) * D],
                                             [h[:, k, c * P:(c + 1) * P] for h in (hh, hl)],
                                             [w[:, k, :] for w in wm2], k == 0, k == KF - 1)
                        mm.then_inc(banks.full(key), 1)

        @block.scalar
        def _(act):
            def affine(b, ring, tiles, keys):
                for k, key in enumerate(keys):
                    act.wait_ge(ring.full(key), ring.filled(b, key))
                    nc.scalar.activation(af[:, k, :], tiles[ring.slot(key)][:], ACT.Identity,
                                         bias=lnb[:, k:k + 1], scale=lnw[:, k:k + 1]).then_inc(ring.free(key), 1)

            def front(b, u):
                affine(b, h_eb, eb, [(u, "nT", k) for k in range(KD)])
                key = (u, "dt")
                act.wait_ge(h_eb.full(key), h_eb.filled(b, key))
                v = eb[h_eb.slot(key)][:, 0:P]
                nc.scalar.activation(dabs[:], v, ACT.Abs, bias=dtb[:]).then_inc(c_dabs.sem, 1)
                nc.scalar.activation(drelu[:], v, ACT.Relu, bias=dtb[:]).then_inc(h_eb.free(key), 1)
                act.wait_ge(c_dabs.sem, c_dabs.at(b, u + 1))
                nc.scalar.activation(dexp[:], dabs[:], ACT.Exp, scale=-1.0).then_inc(c_dexp.sem, 1)

            front(0, 0)
            with act.Fori(0, B) as b:
                for u in us:
                    act.wait_ge(c_cum.sem, c_cum.at(b, u + 1))
                    nc.scalar.activation(cend[:], cum[:, P - 1:P], ACT.Exp)
                    nc.scalar.activation(wexp[:], cum[:], ACT.Exp, bias=cum[:, P - 1:P], scale=-1.0)\
                        .then_inc(c_wexp.sem, 1)
                    for m in PROJ[:XM]:
                        key = (u, "in", m)
                        act.wait_ge(banks.full(key), banks.filled(b, key))
                        nc.scalar.activation(cacc[m - QI][:], bank[banks.slot(key)][:], ACT.Identity,
                                             bias=cb[:, m - QI:m - QI + 1], scale=cw[:, m - QI, TAPS - 1:TAPS])
                        nc.scalar.activation(cin[:, m - QI, TAPS - 1:], bank[banks.slot(key)][:], ACT.Copy)\
                            .then_inc(banks.free(key), 1)
                    for m in PROJ[XM:]:
                        key = (u, "in", m)
                        act.wait_ge(banks.full(key), banks.filled(b, key))
                        nc.scalar.activation(sz[:, m, :], bank[banks.slot(key)][:], ACT.Silu)\
                            .then_inc(banks.free(key), 1)
                    for m in (*range(POOL_CONV, XM), *range(POOL_CONV)):
                        if m < POOL_CONV:
                            act.wait_ge(c_pacc.sem, c_pacc.at(b, POOL_CONV * u + m + 1))
                        else:
                            act.wait_ge(c_cacc.sem, c_cacc.at(b, (XM - POOL_CONV) * (u + 1) - XM + m + 1))
                        nc.scalar.activation(xc[:, m, :], cacc[m][:], ACT.Silu).then_inc(c_xc.sem, 1)
                    for q in range(QI):
                        key = (u, "ec", q)
                        act.wait_ge(banks.full(key), banks.filled(b, key))
                        nc.scalar.activation(ec[:, q, :], bank[banks.slot(key)][:], ACT.Exp)\
                            .then_inc(banks.free(key), 1)

                    def y_out(c):
                        act.wait_ge(c_yg.sem, c_yg.at(b, NC * u + c + 1))
                        last = (u, "op", c - 1) if c else None
                        if last:
                            act.wait_ge(banks.full(last), banks.filled(b, last))
                        nc.scalar.activation(yh[:], yg[:], ACT.Copy).then_inc(c_yh.sem, 1)
                        nc.scalar.activation(ysq[:], yg[:], ACT.Square).then_inc(c_ysq.sem, 1)

                    for n in range(NC * NG + 1):
                        c, i = divmod(n, NG)
                        if c < NC:
                            key = (u, c, i)
                            act.wait_ge(h_eb.full(key), h_eb.filled(b, key))
                            act.wait_ge(h_mh.full(key), h_mh.filled_before(b, key))
                            nc.scalar.activation(es[i % RING].rearrange("s h t -> s (h t)"), eb[h_eb.slot(key)][:],
                                                 ACT.Relu, scale=-1.0).then_inc(h_eb.free(key), 1)
                        if n:
                            key = (u, *divmod(n - 1, NG))
                            act.wait_ge(h_eb.free(key), h_eb.used(b, key))
                            e = es[(i - 1) % RING]
                            nc.scalar.activation(e, e, ACT.Exp, scale=-1.0).then_inc(h_es.full(key), 1)
                        if i == 4 and 0 < c < NC:
                            y_out(c - 1)
                    y_out(NC - 1)

                    affine(b, banks, bank, [(u, "mT", k) for k in range(KD)])
                    for m in range(KF):
                        key = (u, "m1", m)
                        act.wait_ge(banks.full(key), banks.filled(b, key))
                        if m >= HF:
                            act.wait_ge(c_hl.sem, c_hl.at(b, KF * u + m - HF + 1))
                        nc.scalar.activation(hf[m % HF][:], bank[banks.slot(key)][:], ACT.Relu,
                                             bias=b1c[:, m:m + 1]).then_inc(banks.free(key), 1)
                    front(*after_block(b, u))

        @block.gpsimd
        def _(pool):
            def power(b, u, turn, t, v, n):
                pool.wait_ge(c_stat.sem, c_stat.at(b, (3 + NC) * u + turn))
                pool.tensor_tensor(t, v, neg_half[:, 0:n], ALU.pow).then_inc(c_rstd.sem, 1)

            def high(b, u, ring, name):
                for k in range(KD):
                    pool.wait_ge(ring.free((u, name, k)), ring.used(b, (u, name, k)))
                    pool.sem_inc(s_fill, 1)
                    pool.tensor_scalar(ah[:, k, :], af[:, k, :], 1.0, 0.0, ALU.mult, ALU.add)\
                        .then_inc(c_ah.sem, 1)

            power(0, 0, 1, rstd[:], var[:], NC)
            power(0, 0, 2, rstd[:], var[:], NC)
            high(0, 0, h_eb, "nT")
            with pool.Fori(0, B) as b:
                for u in us:
                    pool.wait_ge(c_cum.sem, c_cum.at(b, u + 1))
                    pool.sem_inc(s_fill, 1)
                    for c in range(NC):
                        for j in range(3):
                            last = pool.tensor_copy(cleft[NH * j:NH * (j + 1), c, :],
                                                    parts[NH * c:NH * (c + 1), j, :])
                    last.then_inc(c_left.sem, 1)
                    pool.wait_ge(c_left.sem, c_left.at(b, u + 1))
                    for m in range(POOL_CONV):
                        key = (u, "in", QI + m)
                        pool.wait_ge(banks.free(key), banks.used(b, key))
                        for t in range(TAPS - 1):
                            n = (2 * TAPS - 3) * (POOL_CONV * u + m) + 2 * t
                            pool.sem_inc(s_fill, 1)
                            pool.tensor_scalar(xw[t % 2][:], cin[:, m, t:t + HALF], cw[:, m, t:t + 1], 0.0,
                                               ALU.mult, ALU.add).then_inc(c_ptap.sem, 1)
                            pool.wait_ge(c_ptap.sem, c_ptap.at(b, n + 1))
                            ins = pool.tensor_tensor(cacc[m][:], cacc[m][:], xw[t % 2][:], ALU.add)
                            if t < TAPS - 2:
                                ins.then_inc(c_ptap.sem, 1)
                                pool.wait_ge(c_ptap.sem, c_ptap.at(b, n + 2))
                        ins.then_inc(c_pacc.sem, 1)
                        pool.wait_ge(c_pacc.sem, c_pacc.at(b, POOL_CONV * u + m + 1))
                    for c in range(NC):
                        key = (u, c)
                        pool.wait_ge(c_yread.sem, c_yread.at(b, NC * u + c + 1))
                        if key != (0, 0):
                            pool.wait_ge(h_yoff.free(key), h_yoff.used(b, key))
                        if c:
                            pool.wait_ge(h_yhl.full((u, c - 1)), h_yhl.filled(b, (u, c - 1)))
                        if (u, c) != (0, 0):
                            pool.tensor_tensor(yg[:], yin_s[:], yoff_s[:], ALU.add).then_inc(c_yused.sem, 1)
                            pool.wait_ge(c_yused.sem, c_yused.at(b, NC * u + c + 1))
                            pool.tensor_tensor(yg[:], yg[:], sz[:, :, c * P:(c + 1) * P], ALU.mult)\
                                .then_inc(c_yg.sem, 1)
                        else:
                            pool.sem_inc(s_fill, 1)
                            pool.tensor_copy(yg[:], yin_s[:]).then_inc(c_yused.sem, 1)
                            pool.wait_ge(c_yused.sem, c_yused.at(b, NC * u + c + 1))
                            pool.tensor_tensor(yg[:], yg[:], sz[:, :, c * P:(c + 1) * P], ALU.mult)\
                                .then_inc(c_yg.sem, 1)
                        if c:
                            power(b, u, 2 + c, rms[:], ms[:], 1)
                        if c < NC - 1:
                            pool.wait_ge(c_yh.sem, c_yh.at(b, NC * u + c + 1))
                            pool.tensor_tensor(yl[:], yg[:], yh[:].bitcast(F32), ALU.subtract)\
                                .then_inc(h_yhl.full(key), 1)
                    power(b, u, 2 + NC, rms[:], ms[:], 1)
                    power(b, u, 3 + NC, rstd[:], var[:], NC)
                    following = after_block(b, u)
                    power(*following, 1, rstd[:], var[:], NC)
                    high(b, u, banks, "mT")
                    for m in range(KF):
                        pool.wait_ge(banks.free((u, "m1", m)), banks.used(b, (u, "m1", m)))
                        pool.sem_inc(s_fill, 1)
                        pool.tensor_scalar(hh[:, m, :], hf[m % HF][:], 1.0, 0.0, ALU.mult, ALU.add)\
                            .then_inc(c_hh.sem, 1)
                        if m == 1:
                            power(*following, 2, rstd[:], var[:], NC)
                        if m == 3:
                            pool.wait_ge(c_norm.sem, c_norm.at(b, 2 * u + 2))
                            for c in range(NC):
                                last = pool.tensor_tensor(o1[:, c, :], o1[:, c, :], b2r[:], ALU.add)
                            last.then_inc(c_o1.sem, 1)
                    high(*following, h_eb, "nT")

        @block.vector
        def _(dve):
            def powered(b, u, turn):
                dve.wait_ge(c_rstd.sem, c_rstd.at(b, (3 + NC) * u + turn))

            def normalise(dst, src, b, u, turn, settled):
                for c in range(NC):
                    last = dve.bn_stats(stats[:, c, :], src[:, c, :])
                settled(last)
                dve.sem_inc(s_const, 1)
                for c in range(NC):
                    last = dve.bn_aggr(mv[:, c, :], stats[:, c, :])
                settled(last)
                dve.tensor_scalar(var[:], mv[:, :, 1], EPS, None, ALU.add).then_inc(c_stat.sem, 1)
                powered(b, u, turn)
                for c in range(NC):
                    last = dve.tensor_scalar(dst[:, c, :], src[:, c, :], mv[:, c, 0:1], rstd[:, c:c + 1],
                                             ALU.subtract, ALU.mult)
                return last

            def front(b, u, part):
                turn = [FRONT_STEPS * u + (0, 3, 4, 5, 7)[part]]

                def settled(ins):
                    turn[0] += 1
                    ins.then_inc(own_front.sem, 1)
                    dve.wait_ge(own_front.sem, own_front.at(b, turn[0]))

                if part == 0:
                    dve.wait_ge(xin.full(u), xin.filled(b, u))
                    settled(normalise(res, xs[u], b, u, 1, settled))
                elif part == 1:
                    if u == 0:
                        dve.wait_ge(h_shsc.full(0), h_shsc.filled(b, 0))
                    settled(dve.tensor_tensor(res[:], res[:], shsc[:, 1:2, :].to_broadcast([P, NC, D]), ALU.mult))
                elif part == 2:
                    settled(dve.tensor_tensor(res[:], res[:], shsc[:, 0:1, :].to_broadcast([P, NC, D]), ALU.add))
                elif part == 3:
                    normalise(nrm, res, b, u, 2, settled).then_inc(c_norm.sem, 1)
                else:
                    dve.wait_ge(c_dexp.sem, c_dexp.at(b, u + 1))
                    settled(dve.tensor_scalar(dden[:], dexp[:], 2.0, None, ALU.add))
                    settled(dve.reciprocal(dden[:], dden[:]))
                    settled(dve.tensor_tensor(ds_[:], dexp[:], dden[:], ALU.mult))
                    settled(dve.tensor_tensor(dsq[:], ds_[:], ds_[:], ALU.mult))
                    settled(dve.tensor_scalar(dser[:], dsq[:], 1.0 / (2 * SERIES + 1), None, ALU.mult))
                    for i in range(SERIES - 1, 0, -1):
                        settled(dve.scalar_tensor_tensor(out=dser[:], in0=dser[:], scalar=1.0 / (2 * i + 1),
                                                        in1=dsq[:], op0=ALU.add, op1=ALU.mult))
                    settled(dve.scalar_tensor_tensor(out=dser[:], in0=dser[:], scalar=1.0, in1=ds_[:],
                                                    op0=ALU.add, op1=ALU.mult))
                    settled(dve.scalar_tensor_tensor(out=dtv[:], in0=dser[:], scalar=2.0, in1=drelu[:],
                                                    op0=ALU.mult, op1=ALU.add))
                    settled(dve.tensor_scalar(da[:], dtv[:], nega[:], None, ALU.mult))
                    settled(dve.tensor_tensor_scan(cum[:], ones[:], da[:], 0.0, ALU.mult, ALU.add))
                    settled(dve.tensor_copy(parts[:, 0, :], cum[:]))
                    settled(dve.tensor_tensor(crest[:, 0, :], cum[:], parts[:, 0, :], ALU.subtract))
                    settled(dve.tensor_copy(parts[:, 1, :], crest[:, 0, :]))
                    settled(dve.tensor_tensor(crest[:, 1, :], crest[:, 0, :], parts[:, 1, :], ALU.subtract))
                    dve.tensor_copy(parts[:, 2, :], crest[:, 1, :]).then_inc(c_cum.sem, 1)

            def low(b, u, i, ring, name):
                for k in range(KD):
                    dve.wait_ge(ring.free((u, name, k)), ring.used(b, (u, name, k)))
                    dve.wait_ge(c_ah.sem, c_ah.at(b, KD * (2 * u + i) + k + 1))
                    dve.tensor_tensor(al[:, k, :], af[:, k, :], ah[:, k, :].bitcast(F32), ALU.subtract)\
                        .then_inc(c_al.sem, 1)

            for part in range(5):
                front(0, 0, part)
                if part == 3:
                    low(0, 0, 0, h_eb, "nT")
            with dve.Fori(0, B) as b:
                def mark(ins):
                    return own_dve.mark(ins)

                def after(n):
                    dve.wait_ge(own_dve.sem, own_dve.at(b, n))

                for u in us:
                    dve.wait_ge(c_wexp.sem, c_wexp.at(b, u + 1))
                    mark(dve.tensor_scalar(dend[:], ident[:], cend[:], None, ALU.mult))
                    dve.tensor_tensor(wv[:], wexp[:], dtv[:], ALU.mult).then_inc(c_wv.sem, 1)

                    for m in range(POOL_CONV, XM):
                        key = (u, "in", QI + m)
                        dve.wait_ge(banks.free(key), banks.used(b, key))
                        for t in range(TAPS - 1):
                            ins = dve.scalar_tensor_tensor(
                                out=cacc[m][:], in0=cin[:, m, t:t + HALF], scalar=cw[:, m, t:t + 1],
                                in1=cacc[m][:], op0=ALU.mult, op1=ALU.add)
                            if t < TAPS - 2:
                                after(mark(ins))
                        ins.then_inc(c_cacc.sem, 1)
                        n = (XM - POOL_CONV) * (u + 1) - XM + m + 1
                        dve.wait_ge(c_cacc.sem, c_cacc.at(b, n))
                    dve.wait_ge(c_pacc.sem, c_pacc.at(b, POOL_CONV * (u + 1)))
                    tail = cin[:, :, 0:TAPS - 1]
                    if u < NU - 1:
                        dve.tensor_copy(tail, cin[:, :, HALF:])
                    else:
                        dve.memset(tail, 0.0)

                    key = (u, "dtw")
                    dve.wait_ge(banks.full(key), banks.filled(b, key))
                    dve.tensor_copy(dtw[:].rearrange("s w c h -> s (w c h)"), bank[banks.slot(key)][:, 0:2 * P])\
                        .then_inc(banks.free(key), 1)
                    dve.wait_ge(banks.free(key), banks.used(b, key))
                    key = (u, "dec")
                    dve.wait_ge(banks.full(key), banks.filled(b, key))
                    dve.tensor_copy(dec[:].rearrange("n c h -> n (c h)"), bank[banks.slot(key)][:, 0:P])\
                        .then_inc(banks.free(key), 1)

                    def by_token(c):
                        key = (u, "xT", c)
                        dve.wait_ge(banks.full(key), banks.filled(b, key))
                        xt = bank[banks.slot(key)][:].rearrange("s (h d) -> s h d", d=HD)
                        for w in range(2):
                            dve.tensor_tensor(xpad[c % 2][:, :, w, w, :],
                                              xt.rearrange("s (h w) d -> s h w d", w=2)[:, :, w, :],
                                              dtw[:, 0, c, w::2].unsqueeze(2).to_broadcast([P, NH // 2, HD]), ALU.mult)
                        dve.tensor_tensor(xw[c % 2][:].rearrange("s (h d) -> s h d", d=HD), xt,
                                          dtw[:, 1, c, :].unsqueeze(2).to_broadcast([P, NH, HD]), ALU.mult)\
                            .then_inc(banks.free(key), 1)
                        key = (u, "bt", c)
                        dve.wait_ge(banks.full(key), banks.filled(b, key))
                        dve.tensor_copy(bt[c % 2][:], bank[banks.slot(key)][:, 0:P])
                        dve.tensor_tensor(gm[c % 2][:], bank[banks.slot(key)][:, P:2 * P], tri[:], ALU.mult)\
                            .then_inc(banks.free(key), 1)

                    def addends(c):
                        key, t = (u, c), slice(c * P, (c + 1) * P)
                        dve.wait_ge(c_yused.sem, c_yused.at(b, NC * u + c))
                        last = (u, c, NG - 1)
                        dve.wait_ge(h_mh.free(last), h_mh.used(b, last))
                        for q in range(QI):
                            ins = dve.scalar_tensor_tensor(out=yin_s[:, q, :], in0=xc[:, q, t], scalar=dsk[:, q:q + 1],
                                                           in1=yin[:, q, :], op0=ALU.mult, op1=ALU.add)
                        ins.then_inc(c_yread.sem, 1)
                        if key != (0, 0):
                            dve.wait_ge(h_yoff.full(key), h_yoff.filled(b, key))
                            for q in range(QI):
                                dve.wait_ge(banks.free((u, "ec", q)), banks.used(b, (u, "ec", q)))
                            if c:
                                dve.wait_ge(c_ysum.sem, c_ysum.at(b, NC * u + c))
                            dve.tensor_tensor(yoff_s[:], yoff[:], ec[:, :, t], ALU.mult).then_inc(h_yoff.free(key), 1)
                    def y_halves(c):
                        key = (u, c)
                        if c == NC - 1:
                            dve.wait_ge(c_yh.sem, c_yh.at(b, NC * u + c + 1))
                            dve.tensor_tensor(yl[:], yg[:], yh[:].bitcast(F32), ALU.subtract)\
                                .then_inc(h_yhl.full(key), 1)
                        dve.wait_ge(c_ysq.sem, c_ysq.at(b, NC * u + c + 1))
                        dve.tensor_reduce(ysum[:], ysq[:].rearrange("d q t -> d t q"), AX.X, ALU.add)\
                            .then_inc(c_ysum.sem, 1)

                    def square_mean(c):
                        key = (u, "op", c)
                        dve.wait_ge(banks.full(key), banks.filled(b, key))
                        dve.tensor_scalar(ms[:], bank[banks.slot(key)][:, D:D + 1], 1.0 / DI, EPS,
                                          ALU.mult, ALU.add).then_inc(c_stat.sem, 1)

                    def residual(c):
                        key = (u, "op", c)
                        powered(b, u, 3 + c)
                        dve.scalar_tensor_tensor(out=o1[:, c, :], in0=bank[banks.slot(key)][:, 0:D], scalar=rms[:],
                                                 in1=res[:, c, :], op0=ALU.mult, op1=ALU.add)\
                            .then_inc(banks.free(key), 1)

                    def new_state(c):
                        key = (u, "st", c)
                        dve.wait_ge(banks.full(key), banks.filled(b, key))
                        if (u, c) == (0, 0):
                            dve.tensor_copy(state[:], bank[banks.slot(key)][:]).then_inc(banks.free(key), 1)
                        else:
                            s3 = state[:].rearrange("n (h d) -> n h d", d=HD)
                            dve.wait_ge(banks.free((u, "dec")), banks.used(b, (u, "dec")))
                            after(mark(dve.tensor_tensor(s3, s3, dec[:, c, :].unsqueeze(2).to_broadcast([P, NH, HD]),
                                                         ALU.mult)))
                            dve.tensor_tensor(state[:], state[:], bank[banks.slot(key)][:], ALU.add)\
                                .then_inc(banks.free(key), 1)
                        dve.wait_ge(banks.free(key), banks.used(b, key))

                    by_token(0)
                    for c in range(NC):
                        dve.wait_ge(banks.free((u, "bt", c)), banks.used(b, (u, "bt", c)))
                        for i in range(NG):
                            key = (u, c, i)
                            dve.wait_ge(h_es.full(key), h_es.filled(b, key))
                            dve.wait_ge(h_mh.free(key), h_mh.used_before(b, key))
                            dve.tensor_tensor(mh[i % RING][:], es[i % RING],
                                              gm[c % 2][:].unsqueeze(1).to_broadcast([P, G4, P]),
                                              ALU.mult).then_inc(h_mh.full(key), 1)
                            if i == 1 and c:
                                addends(c - 1)
                            if i == 3 and c >= 2:
                                square_mean(c - 2)
                            if i == 4 and c >= 2:
                                residual(c - 2)
                            if i == 4 and c + 1 < NC:
                                by_token(c + 1)
                            if i == 6 and c:
                                y_halves(c - 1)
                            if i == 7:
                                new_state(c)
                    addends(NC - 1)
                    square_mean(NC - 2)
                    residual(NC - 2)
                    y_halves(NC - 1)
                    square_mean(NC - 1)
                    residual(NC - 1)

                    dve.wait_ge(banks.free((u, "op", NC - 1)), banks.used(b, (u, "op", NC - 1)))
                    normalise(nrm, o1, b, u, 3 + NC, lambda ins: after(mark(ins))).then_inc(c_norm.sem, 1)
                    following = after_block(b, u)
                    front(*following, 0)
                    low(b, u, 1, banks, "mT")
                    front(*following, 1)
                    front(*following, 2)
                    for m in range(KF):
                        dve.wait_ge(c_hh.sem, c_hh.at(b, KF * u + m + 1))
                        dve.tensor_tensor(hl[:, m, :], hf[m % HF][:], hh[:, m, :].bitcast(F32), ALU.subtract)\
                            .then_inc(c_hl.sem, 1)
                        if m == 1:
                            front(*following, 3)
                    low(*following, 0, h_eb, "nT")
                    front(*following, 4)
                    dve.wait_ge(c_o1.sem, c_o1.at(b, u + 1))
                    if u == 0:
                        dve.wait_ge(h_gate.full(0), h_gate.filled(b, 0))
                    for j in range(NC // 2):
                        key, cc = (u, "m2", j), slice(2 * j, 2 * j + 2)
                        dve.wait_ge(banks.full(key), banks.filled(b, key))
                        dve.tensor_tensor(o1[:, cc, :], o1[:, cc, :],
                                          bank[banks.slot(key)][:].rearrange("p (c d) -> p c d", c=2), ALU.add)\
                            .then_inc(banks.free(key), 1)
                        dve.wait_ge(banks.free(key), banks.used(b, key))
                    after(mark(dve.tensor_tensor(o1[:], o1[:], gate[:].unsqueeze(1).to_broadcast([P, NC, D]),
                                                 ALU.mult)))
                    dve.tensor_tensor(xs[u][:], xs[u][:], o1[:], ALU.add).then_inc(c_x1.sem, 1)
            own_dve.closed()


FFN_BANKS = 6


def feed_forward(nc, ctx, sem, g):
    ident, ones, neg_half = g["ident"], g["ones"], g["neg_half"]
    mod_d, x1_d = g["mod_d"], g["x1_d"]
    s_fill, s_const = g["s_fill"], g["s_const"]

    def sb(name, shape, dt=F32):
        return ctx.enter_context(nc.sbuf_tensor(name, shape, dt))

    shapes = ((KD, FF), (KD, FF), (KF, FF), (KF, FF), (KF, D))
    ws = [sb(f"fw{i}", [P, k, n], F32R) for i, (k, n) in enumerate(shapes)]
    s1 = sb("s1", [P, KF])
    s2 = sb("s2", [P, KF])
    sh1 = sb("sh1", [P, KF])
    sh2 = sb("sh2", [P, KF])
    s3r = sb("s3r", [P, D])
    inexact = sb("inexact", [1, 1], I32)
    fx = [sb(f"fx{u}", [P, NC, D]) for u in range(NU)]
    csc = sb("csc", [P, KD])
    csh = sb("csh", [P, KD])
    gb = sb("gb", [P, D])
    stats = sb("fstats", [P, NC, 6])
    mv = sb("fmv", [P, NC, 2])
    var = sb("fvar", [P, NC])
    rstd = sb("frstd", [P, NC])

    us = range(NU)
    layers = ("g", "h1", "h2")
    banks = Handover(sem, "fbank", list(ffn_bank_order()), FFN_BANKS)
    fronts = Handover(sem, "front", [(u, k) for u in us for k in range(KD)], KD)
    xin = Handover(sem, "fx", list(us), 2, fills=16, uses=16)
    c_mod = Count(sem, "fmod_loaded", 32)
    c_gbin = Count(sem, "gb_loaded", 16)
    c_stat = Count(sem, "fvariance_made", NU)
    c_rstd = Count(sem, "frstd_made", NU)
    c_norm = Count(sem, "fnorm_made", NU)
    c_ah = Count(sem, "fact_hi_made", NU)
    c_al = Count(sem, "fact_lo_made", NU)
    c_hi = Count(sem, "fhidden_hi_made", NU * 3 * KF)
    c_lo = Count(sem, "fhidden_lo_made", NU * 3 * KF)
    c_gb = Count(sem, "gb_made", 1)
    c_out = Count(sem, "out_made", NU)
    c_bn = Count(sem, "fstats_made", 2 * NU)
    s_passed = sem("fpassed")
    counts = [v for v in locals().values() if isinstance(v, (Handover, Count))]

    with ExitStack() as own:
        PIECE = 2048
        rounded = [own.enter_context(nc.sbuf_tensor(f"rounded{j}", [P, PIECE], F32R)) for j in range(2)]
        differs = own.enter_context(nc.sbuf_tensor("differs", [P, PIECE], F32))
        pieces = [(i, o, min(PIECE, k * n - o)) for i, (k, n) in enumerate(shapes) for o in range(0, k * n, PIECE)]
        count = own.enter_context(nc.sbuf_tensor("count", [P, len(pieces)], F32))
        total = own.enter_context(nc.sbuf_tensor("total", [P, 1], F32))
        sum_p = own.enter_context(nc.psum_tensor("sum_p", [1, 1], F32))
        s_w = [sem(f"s_ffn_w{i}") for i in range(len(shapes))]
        s_vec = sem("s_ffn_vec")
        s_round = sem("s_rounded")
        s_count = sem("s_counted")
        s_sum = sem("s_summed")
        s_flag = sem("s_flag")
        block = own.enter_context(nc.Block())

        @block.sync
        def _(sp):
            for i, w in enumerate(ws):
                sp.dma_start(w[:].rearrange("p k n -> p (k n)").bitcast(F32), g["ffn_d"][i]).then_inc(s_w[i], 16)
            start(sp, counts)
            with nc.allow_non_contiguous_dma(reason="a few small vectors"):
                for dst, name in ((s1, "s1"), (s2, "s2"), (sh1, "sh1"), (sh2, "sh2")):
                    sp.dma_start(dst[:], rows(g[name], P)).then_inc(s_vec, 16)
            sp.dma_start(s3r[:], g["s3"].partition_broadcast(P)).then_inc(s_vec, 16)
            sp.wait_ge(s_vec, 80)

        @block.scalar
        def _(act):
            for n, (i, o, size) in enumerate(pieces):
                if o == 0:
                    act.wait_ge(s_w[i], 16)
                if n >= 2:
                    act.wait_ge(s_count, n - 1)
                w = ws[i][:].rearrange("p k n -> p (k n)").bitcast(F32)[:, o:o + size]
                nc.scalar.activation(rounded[n % 2][:, 0:size], w, ACT.Copy).then_inc(s_round, 1)

        @block.vector
        def _(dve):
            for n, (i, o, size) in enumerate(pieces):
                w = ws[i][:].rearrange("p k n -> p (k n)").bitcast(F32)[:, o:o + size]
                dve.wait_ge(s_round, n + 1)
                if n:
                    dve.wait_ge(s_count, n)
                dve.scalar_tensor_tensor(out=differs[:, 0:size], in0=w, scalar=0.0,
                                         in1=rounded[n % 2][:, 0:size].bitcast(F32), op0=ALU.add,
                                         op1=ALU.not_equal, accum_out=count[:, n:n + 1]).then_inc(s_count, 1)
            dve.wait_ge(s_count, len(pieces))
            dve.tensor_reduce(total[:], count[:], AX.X, ALU.add).then_inc(s_count, 1)
            dve.wait_ge(s_sum, 1)
            dve.tensor_copy(inexact[:], sum_p[:]).then_inc(s_flag, 1)

        @block.tensor
        def _(pe):
            pe.wait_ge(s_count, len(pieces) + 1)
            pe.matmul(sum_p[:], total[:], ones[:, 0:1], start=True, stop=True).then_inc(s_sum, 1)

    nrm = sb("fnrm", [P, NC, D])
    go = sb("go", [P, NC, D])
    af = sb("faf", [P, KD, HALF])
    ah = sb("fah", [P, KD, HALF], F32R)
    al = sb("fal", [P, KD, HALF], F32R)
    sa = [sb(f"sa{j}", [P, HALF]) for j in range(2)]
    hf = [sb(f"fhf{j}", [P, HALF]) for j in range(3)]
    hid = [[sb(f"hid{s}{j}", [P, KF, HALF], F32R) for j in range(2)] for s in range(2)]

    with ExitStack() as own:
        bank = [own.enter_context(nc.psum_tensor(f"fbank{j}", [P, 512], F32)) for j in range(FFN_BANKS)]
        front = [own.enter_context(nc.psum_tensor(f"front{j}", [P, 512], F32)) for j in range(KD)]
        block = own.enter_context(nc.Block())

        @block.sync
        def _(sp):
            def load(b, u, row):
                sp.wait_ge(xin.free(u), xin.used_before(b, u))
                sp.sem_inc(s_passed, 1)
                sp.dma_start(fx[u][:], x1_d[row, u * HALF:(u + 1) * HALF, :].rearrange(
                    "(c p) d -> p c d", p=P)).then_inc(xin.full(u), 16)
                if u == 0:
                    with nc.allow_non_contiguous_dma(reason="two small vectors"):
                        sp.dma_start(csh[:], rows(mod_d[row, 3 * D:4 * D], P)).then_inc(c_mod.sem, 16)
                        sp.dma_start(csc[:], rows(mod_d[row, 4 * D:5 * D], P)).then_inc(c_mod.sem, 16)

            load(0, 0, 0)
            with sp.Fori(0, B) as b:
                next_row = sp.snap((b + 1) % B)
                for u in us:
                    nb, nu = after_block(b, u)
                    if u == 0:
                        sp.wait_ge(c_out.sem, c_out.at(b, 0))
                        sp.sem_inc(s_passed, 1)
                        sp.dma_start(gb[:], mod_d[b, 5 * D:6 * D].partition_broadcast(P)).then_inc(c_gbin.sem, 16)
                    if nu == 0:
                        for k in range(KD):
                            sp.wait_ge(fronts.free((u, k)), fronts.used(b, (u, k)))
                    load(nb, nu, b if nu else next_row)
                    sp.wait_ge(c_out.sem, c_out.at(b, u + 1))
                    sp.sem_inc(s_passed, 1)
                    sp.dma_start(g["out"][b, u * HALF:(u + 1) * HALF, :].rearrange("(c p) d -> p c d", p=P),
                                 fx[u][:]).then_inc(xin.free(u), 16)
            for u in us:
                sp.wait_ge(xin.free(u), 16 * B + START)

        @block.tensor
        def _(pe):
            def rows_of_batch(dt):
                def layer(b, u, name, w, halves, wait):
                    for m in range(KF):
                        key = (u, name, m)
                        pe.wait_ge(banks.free(key), banks.used_before(b, key))
                        for k in range(w.shape[1]):
                            if m == 0 and wait is not None:
                                pe.wait_ge(c_lo.sem, c_lo.at(b, wait + k + 1))
                            for n, h in enumerate(halves):
                                mm = pe.matmul(bank[banks.slot(key)][:], w[:, k, m * P:(m + 1) * P].bitcast(dt),
                                               h[:, k, :].bitcast(dt), start=(k + n == 0),
                                               stop=(k == w.shape[1] - 1 and n == 1))
                        mm.then_inc(banks.full(key), 1)

                def transposes(b, u):
                    pe.wait_ge(c_norm.sem, c_norm.at(b, u + 1))
                    for k in range(KD):
                        pe.wait_ge(fronts.free((u, k)), fronts.used_before(b, (u, k)))
                        for c in range(NC):
                            mm = pe.transpose(front[k][:, c * P:(c + 1) * P], nrm[:, c, k * P:(k + 1) * P], ident[:])
                        mm.then_inc(fronts.full((u, k)), 1)

                transposes(0, 0)
                with pe.Fori(0, B) as b:
                    for u in us:
                        pe.wait_ge(c_al.sem, c_al.at(b, u + 1))
                        for m in range(KF):
                            for name, w in (("a", ws[0]), ("g", ws[1])):
                                key = (u, name, m)
                                pe.wait_ge(banks.free(key), banks.used_before(b, key))
                                for k in range(KD):
                                    for n, h in enumerate((ah, al)):
                                        mm = pe.matmul(bank[banks.slot(key)][:],
                                                       w[:, k, m * P:(m + 1) * P].bitcast(dt), h[:, k, :].bitcast(dt),
                                                       start=(k + n == 0), stop=(k == KD - 1 and n == 1))
                                mm.then_inc(banks.full(key), 1)
                        at = 3 * KF * u
                        layer(b, u, "h1", ws[2], hid[0], at)
                        transposes(*after_block(b, u))
                        layer(b, u, "h2", ws[3], hid[1], at + KF)
                        for j in range(NC // 2):
                            key = (u, "o", j)
                            pe.wait_ge(banks.free(key), banks.used_before(b, key))
                            for c in range(2 * j, 2 * j + 2):
                                for k in range(KF):
                                    if c == 0:
                                        pe.wait_ge(c_lo.sem, c_lo.at(b, at + 2 * KF + k + 1))
                                    for n, h in enumerate(hid[0]):
                                        mm = pe.matmul(bank[banks.slot(key)][:, (c % 2) * D:(c % 2 + 1) * D],
                                                       h[:, k, c * P:(c + 1) * P].bitcast(dt),
                                                       ws[4][:, k, :].bitcast(dt), start=(k + n == 0),
                                                       stop=(k == KF - 1 and n == 1))
                            mm.then_inc(banks.full(key), 1)

            differing = pe.value_load(inexact[0:1, 0:1])
            with pe.If(differing == 0):
                rows_of_batch(F32R)
            with pe.Else():
                rows_of_batch(F32)

        @block.scalar
        def _(act):
            def affine(b, u):
                if u == 0:
                    act.wait_ge(c_mod.sem, c_mod.at(b, 32))
                for k in range(KD):
                    act.wait_ge(fronts.full((u, k)), fronts.filled(b, (u, k)))
                    nc.scalar.activation(af[:, k, :], front[k][:], ACT.Identity,
                                         bias=csh[:, k:k + 1], scale=csc[:, k:k + 1]).then_inc(fronts.free((u, k)), 1)

            affine(0, 0)
            with act.Fori(0, B) as b:
                for u in us:
                    for m in range(KF):
                        key = (u, "a", m)
                        act.wait_ge(banks.full(key), banks.filled(b, key))
                        if m >= 2:
                            before = (u, "g", m - 2)
                            act.wait_ge(banks.free(before), banks.used(b, before))
                        nc.scalar.activation(sa[m % 2][:], bank[banks.slot(key)][:], ACT.Silu, scale=s1[:, m:m + 1])\
                            .then_inc(banks.free(key), 1)
                    for i, (name, s) in enumerate((("h1", sh1), ("h2", sh2)), 1):
                        if i == 2:
                            affine(*after_block(b, u))
                        for m in range(KF):
                            key, j = (u, name, m), KF * i + m
                            act.wait_ge(banks.full(key), banks.filled(b, key))
                            act.wait_ge(c_lo.sem, c_lo.at(b, 3 * KF * u + j - 2))
                            nc.scalar.activation(hf[j % 3][:], bank[banks.slot(key)][:], ACT.Gelu,
                                                 scale=s[:, m:m + 1]).then_inc(banks.free(key), 1)

        @block.gpsimd
        def _(pool):
            def power(b, u):
                pool.wait_ge(c_stat.sem, c_stat.at(b, u + 1))
                pool.tensor_tensor(rstd[:], var[:], neg_half[:, 0:NC], ALU.pow).then_inc(c_rstd.sem, 1)

            def high(b, u):
                for k in range(KD):
                    pool.wait_ge(fronts.free((u, k)), fronts.used(b, (u, k)))
                pool.sem_inc(s_fill, 1)
                pool.tensor_scalar(ah[:], af[:], 1.0, 0.0, ALU.mult, ALU.add).then_inc(c_ah.sem, 1)

            power(0, 0)
            high(0, 0)
            with pool.Fori(0, B) as b:
                for u in us:
                    for i, name in enumerate(layers):
                        if i == 2:
                            high(*after_block(b, u))
                        for m in range(KF):
                            if (i, m) == (1, 3):
                                power(*after_block(b, u))
                            j = KF * i + m
                            pool.wait_ge(banks.free((u, name, m)), banks.used(b, (u, name, m)))
                            pool.sem_inc(s_fill, 1)
                            pool.tensor_scalar(hid[i % 2][0][:, m, :], hf[j % 3][:], 1.0, 0.0, ALU.mult, ALU.add)\
                                .then_inc(c_hi.sem, 1)

        @block.vector
        def _(dve):
            def variances(b, u):
                dve.wait_ge(xin.full(u), xin.filled(b, u))
                for c in range(NC):
                    last = dve.bn_stats(stats[:, c, :], fx[u][:, c, :])
                last.then_inc(c_bn.sem, 1)
                dve.wait_ge(c_bn.sem, c_bn.at(b, 2 * u + 1))
                dve.sem_inc(s_const, 1)
                for c in range(NC):
                    last = dve.bn_aggr(mv[:, c, :], stats[:, c, :])
                last.then_inc(c_bn.sem, 1)
                dve.wait_ge(c_bn.sem, c_bn.at(b, 2 * u + 2))
                dve.tensor_scalar(var[:], mv[:, :, 1], EPS, None, ALU.add).then_inc(c_stat.sem, 1)

            def normalise(b, u):
                dve.wait_ge(c_rstd.sem, c_rstd.at(b, u + 1))
                for c in range(NC):
                    last = dve.tensor_scalar(nrm[:, c, :], fx[u][:, c, :], mv[:, c, 0:1], rstd[:, c:c + 1],
                                             ALU.subtract, ALU.mult)
                last.then_inc(c_norm.sem, 1)

            def front_low(b, u):
                for k in range(KD):
                    dve.wait_ge(fronts.free((u, k)), fronts.used(b, (u, k)))
                dve.wait_ge(c_ah.sem, c_ah.at(b, u + 1))
                dve.tensor_tensor(al[:], af[:], ah[:].bitcast(F32), ALU.subtract).then_inc(c_al.sem, 1)

            variances(0, 0)
            normalise(0, 0)
            front_low(0, 0)
            with dve.Fori(0, B) as b:
                for u in us:
                    if u == 0:
                        dve.wait_ge(c_gbin.sem, c_gbin.at(b, 16))
                        dve.tensor_tensor(gb[:], gb[:], s3r[:], ALU.mult).then_inc(c_gb.sem, 1)

                    def low(i, m):
                        j = KF * i + m
                        dve.wait_ge(c_hi.sem, c_hi.at(b, 3 * KF * u + j + 1))
                        dve.tensor_tensor(hid[i % 2][1][:, m, :], hf[j % 3][:], hid[i % 2][0][:, m, :].bitcast(F32),
                                          ALU.subtract).then_inc(c_lo.sem, 1)

                    for m in range(KF):
                        gate_key, key = (u, "a", m), (u, "g", m)
                        dve.wait_ge(banks.free(gate_key), banks.used(b, gate_key))
                        dve.wait_ge(c_lo.sem, c_lo.at(b, max(3 * KF * u + m - 2, 0)))
                        dve.wait_ge(banks.full(key), banks.filled(b, key))
                        dve.scalar_tensor_tensor(out=hf[m % 3][:], in0=bank[banks.slot(key)][:], scalar=s2[:, m:m + 1],
                                                 in1=sa[m % 2][:], op0=ALU.mult, op1=ALU.mult)\
                            .then_inc(banks.free(key), 1)
                        if m:
                            low(0, m - 1)
                    low(0, KF - 1)
                    for i in (1, 2):
                        if i == 2:
                            front_low(*after_block(b, u))
                        for m in range(KF):
                            low(i, m)
                            if (i, m) == (1, 1):
                                variances(*after_block(b, u))
                            if (i, m) == (1, 4):
                                normalise(*after_block(b, u))
                    if u == 0:
                        dve.wait_ge(c_gb.sem, c_gb.at(b, 1))
                    for j in range(NC // 2):
                        key, cc = (u, "o", j), slice(2 * j, 2 * j + 2)
                        dve.wait_ge(banks.full(key), banks.filled(b, key))
                        dve.tensor_tensor(go[:, cc, :], bank[banks.slot(key)][:].rearrange("p (c d) -> p c d", c=2),
                                          gb[:].unsqueeze(1).to_broadcast([P, 2, D]), ALU.mult)\
                            .then_inc(banks.free(key), 1)
                    dve.wait_ge(banks.free(key), banks.used(b, key))
                    dve.wait_ge(banks.free((u, "o", 0)), banks.used(b, (u, "o", 0)))
                    dve.tensor_tensor(fx[u][:], fx[u][:], go[:], ALU.add).then_inc(c_out.sem, 1)


def kernel(**inputs):
    import numpy as np
    import concourse.bacc as bacc
    from concourse.bass_utils import run_bass_kernel_spmd as run

    nc = bacc.Bacc("TRN2", target_bir_lowering=False, num_devices=1)
    a = {k[3:]: np.asarray(v) for k, v in inputs.items()}
    t = np.ascontiguousarray
    arrays = dict(
        x=a["attn_x"], ln_w=a["attn_ln_w"], ln_b=a["attn_ln_b"], w_in=a["attn_in_proj_w"], conv_w=a["attn_conv_w"],
        conv_b=a["attn_conv_b"], dt_bias=a["attn_dt_bias"], a_log=a["attn_A_log"], d_skip=a["attn_D_skip"],
        rms_w=a["attn_rms_w"], w_out=a["attn_out_proj_w"], m1=a["attn_mlp_w1"], b1=a["attn_mlp_b1"],
        m2=a["attn_mlp_w2"], b2=a["attn_mlp_b2"], w1=t(a["ffn_w1_w"].T), s1=a["ffn_w1_s"], w2=t(a["ffn_w2_w"].T),
        s2=a["ffn_w2_s"], h1=t(a["ffn_h1_w"].T), sh1=a["ffn_h1_s"], h2=t(a["ffn_h2_w"].T), sh2=a["ffn_h2_s"],
        w3=t(a["ffn_w3_w"].T), s3=a["ffn_w3_s"], cT=t(a["c"].T), wmod=a["wmod"])
    arrays = {f"in_{k}": t(v) for k, v in arrays.items()}
    args = {k[3:]: nc.dram_tensor(k, v.shape, mybir.dt.from_np(v.dtype), kind="ExternalInput").ap()
            for k, v in arrays.items()}
    out = nc.dram_tensor("out_x", (B, L, D), F32, kind="ExternalOutput").ap()
    build(nc, **args, out=out)
    return run(nc, [arrays], core_ids=[0]).results[0]["out_x"]
```
